# Optimizing a Trainium2 kernel written in Bass

```python
import numpy as np
import jax
import jax.numpy as jnp

def _softmax(x, axis=-1):
    return jax.nn.softmax(x, axis=axis)

def _gelu(x):
    return jax.nn.gelu(x, approximate=True)

def _silu(x):
    return jax.nn.silu(x)

def _sigmoid(x):
    return jax.nn.sigmoid(x)

def _layernorm(x, axis=-1, eps=1e-05):
    m = jnp.mean(x, axis=axis, keepdims=True)
    v = jnp.var(x, axis=axis, keepdims=True)
    return (x - m) / jnp.sqrt(v + eps)

def _scatter_add(tgt, idx, src, axis=0):
    return tgt.at[idx].add(src)

def _segment_sum(src, seg, n):
    return jax.ops.segment_sum(src, seg, n)
kernel_name = 'mk_flamingo_gated_d1_seqx_r8_3b777a'

def setup_inputs(seed: int=0):
    np.random.seed(seed)
    _w = jnp.asarray

    def _rec_inputs():
        import jax
        import jax.numpy as jnp
        _rk = jax.random.key(seed)
        x = 2.818e-05 + 1 * jax.random.normal(jax.random.fold_in(_rk, 1), (4, 256, 128), jnp.float32)
        _lenS = 256 - jax.random.randint(jax.random.fold_in(_rk, 7), (4,), 0, max(1, 256 // 4) + 1, jnp.int32)
        _lenS2 = 256 - jax.random.randint(jax.random.fold_in(_rk, 8), (4,), 0, max(1, 256 // 4) + 1, jnp.int32)
        _ctx_2048P = jax.random.normal(jax.random.fold_in(_rk, 11), (4, 16, 256), jnp.float32)
        _ctx_2048c = jax.random.dirichlet(jax.random.fold_in(_rk, 511), 0.3 * jnp.ones((16,), jnp.float32), (4, 256))
        _ctx_2048t = jnp.einsum('bsk,bkd->bsd', _ctx_2048c, _ctx_2048P)
        _ctx_2048t = _ctx_2048t * jax.lax.rsqrt(jnp.mean(jnp.square(_ctx_2048t)) + 1e-12) * 0.953939
        ctx_2048 = -0.000125008 + 0.999885 * (_ctx_2048t + 0.3 * jax.random.normal(jax.random.fold_in(_rk, 611), (4, 256, 256), jnp.float32))
        _validS = jnp.arange(256)[None, :] < _lenS[:, None]
        _validS2 = jnp.arange(256)[None, :] < _lenS2[:, None]
        _causal = jnp.tril(jnp.ones((256, 256), dtype=bool))
        mask_BxS2_fk1 = jnp.where(jnp.broadcast_to(_validS2[:, :], (4, 256)), 1.0, 0.0).astype(jnp.float32)
        _g = jax.random.normal(jax.random.fold_in(_rk, 9001), (2, 1), jnp.float32)
        _g = jnp.sign(_g) * jnp.maximum(jnp.abs(_g), 1.0) + (_g == 0) * 1.0
        g_xattn = _g[0]
        g_ffn = _g[1]
        return (x, ctx_2048, mask_BxS2_fk1, g_xattn, g_ffn)
    x, ctx_2048, mask_BxS2_fk1, g_xattn, g_ffn = _rec_inputs()

    def _L0_xattn_setup():
        import jax, jax.numpy as jnp
        import numpy as np
        B, S, T = (32, 64, 64)
        SRC_SIZE, TGT_SIZE, OUT_SIZE, NUM_HEAD = (256, 128, 128, 8)
        HEAD_DIM = OUT_SIZE // NUM_HEAD
        key = jax.random.key(seed)
        ks = jax.random.split(key, 12)
        src = jax.random.normal(ks[0], (B, S, SRC_SIZE), dtype=jnp.float32)
        tgt = jax.random.normal(ks[1], (B, T, TGT_SIZE), dtype=jnp.float32)
        src_mask = (jax.random.uniform(ks[2], (B, S)) > 0.3).astype(jnp.float32)
        src_mask = src_mask.at[:, 0].set(1.0)
        tgt_mask = (jax.random.uniform(ks[3], (B, T)) > 0.3).astype(jnp.float32)
        tgt_mask = tgt_mask.at[:, 0].set(1.0)

        def lin(k, out_f, in_f):
            return jax.random.normal(k, (out_f, in_f), dtype=jnp.float32) / np.sqrt(in_f)
        W_src = lin(ks[4], 2 * OUT_SIZE, SRC_SIZE)
        b_src = jnp.zeros((2 * OUT_SIZE,), jnp.float32)
        W_tgt = lin(ks[5], OUT_SIZE, TGT_SIZE)
        b_tgt = jnp.zeros((OUT_SIZE,), jnp.float32)
        W_out = lin(ks[6], OUT_SIZE, OUT_SIZE + TGT_SIZE)
        b_out = jnp.zeros((OUT_SIZE,), jnp.float32)
        return {'src': src, 'tgt': tgt, 'src_mask': src_mask, 'tgt_mask': tgt_mask, 'W_src': W_src, 'b_src': b_src, 'W_tgt': W_tgt, 'b_tgt': b_tgt, 'W_out': W_out, 'b_out': b_out}
    _L0_xattn_all = _L0_xattn_setup()
    _L0_xattn_in = {k: v for k, v in _L0_xattn_all.items() if k in ('W_src', 'b_src', 'W_tgt', 'b_tgt', 'W_out', 'b_out')}
    del _L0_xattn_all

    def _L0_ffn_setup():
        import jax, jax.numpy as jnp
        import numpy as np
        DIM = 128
        HIDDEN = 512
        E = 8
        B, S = (2, 512)
        key = jax.random.key(seed)
        ks = jax.random.split(key, 8)
        sd = 1.0 / np.sqrt(DIM)
        sh = 1.0 / np.sqrt(HIDDEN)
        return {'x': jax.random.normal(ks[0], (B, S, DIM), dtype=jnp.float32), 'router_w': jax.random.uniform(ks[1], (DIM, E), jnp.float32, -sd, sd), 'router_b': jax.random.uniform(ks[2], (E,), jnp.float32, -sd, sd), 'w1': jax.random.uniform(ks[3], (E, DIM, 2 * HIDDEN), jnp.float32, -sd, sd), 'b1': jax.random.uniform(ks[4], (E, 2 * HIDDEN), jnp.float32, -sd, sd), 'w2': jax.random.uniform(ks[5], (E, HIDDEN, DIM), jnp.float32, -sh, sh), 'b2': jax.random.uniform(ks[6], (E, DIM), jnp.float32, -sh, sh)}
    _L0_ffn_all = _L0_ffn_setup()
    _L0_ffn_in = {k: v for k, v in _L0_ffn_all.items() if k in ('router_w', 'router_b', 'w1', 'b1', 'w2', 'b2')}
    del _L0_ffn_all
    return {'x': x, 'ctx_2048': ctx_2048, 'mask_BxS2_fk1': mask_BxS2_fk1, 'g_xattn': g_xattn, 'g_ffn': g_ffn, 'L0_xattn_W_src': _L0_xattn_in['W_src'], 'L0_xattn_b_src': _L0_xattn_in['b_src'], 'L0_xattn_W_tgt': _L0_xattn_in['W_tgt'], 'L0_xattn_b_tgt': _L0_xattn_in['b_tgt'], 'L0_xattn_W_out': _L0_xattn_in['W_out'], 'L0_xattn_b_out': _L0_xattn_in['b_out'], 'L0_ffn_router_w': _L0_ffn_in['router_w'], 'L0_ffn_router_b': _L0_ffn_in['router_b'], 'L0_ffn_w1': _L0_ffn_in['w1'], 'L0_ffn_b1': _L0_ffn_in['b1'], 'L0_ffn_w2': _L0_ffn_in['w2'], 'L0_ffn_b2': _L0_ffn_in['b2']}

def reference(x, ctx_2048, mask_BxS2_fk1, g_xattn, g_ffn, L0_xattn_W_src, L0_xattn_b_src, L0_xattn_W_tgt, L0_xattn_b_tgt, L0_xattn_W_out, L0_xattn_b_out, L0_ffn_router_w, L0_ffn_router_b, L0_ffn_w1, L0_ffn_b1, L0_ffn_w2, L0_ffn_b2):
    import jax
    import jax.numpy as jnp

    def _L0_xattn_ref(src, tgt, src_mask, tgt_mask, W_src, b_src, W_tgt, b_tgt, W_out, b_out):
        import jax, jax.numpy as jnp
        import numpy as np
        B, S, T = (32, 64, 64)
        SRC_SIZE, TGT_SIZE, OUT_SIZE, NUM_HEAD = (256, 128, 128, 8)
        HEAD_DIM = OUT_SIZE // NUM_HEAD
        b, s, _ = src.shape
        t = tgt.shape[1]
        src_trans = jnp.einsum('bsf,of->bso', src, W_src) + b_src
        tgt_trans = jnp.einsum('btf,of->bto', tgt, W_tgt) + b_tgt
        src_trans = src_trans * src_mask[:, :, None]
        tgt_trans = tgt_trans * tgt_mask[:, :, None]
        src_key, src_val = jnp.split(src_trans, 2, axis=2)
        k = src_key.reshape(b, s, NUM_HEAD, HEAD_DIM)
        v = src_val.reshape(b, s, NUM_HEAD, HEAD_DIM)
        q = tgt_trans.reshape(b, t, NUM_HEAD, HEAD_DIM)
        scores = jnp.einsum('bthd,bshd->bhts', q, k) / np.sqrt(HEAD_DIM)
        scores = jnp.where(src_mask[:, None, None, :] == 0, -jnp.inf, scores)
        attn = jax.nn.softmax(scores, axis=-1)
        tgt_update = jnp.einsum('bhts,bshd->bthd', attn, v).reshape(b, t, OUT_SIZE)
        cat_tgt = jnp.concatenate([tgt, tgt_update], axis=2)
        return jnp.einsum('btf,of->bto', cat_tgt, W_out) + b_out

    def _L0_ffn_ref(x, router_w, router_b, w1, b1, w2, b2):
        import jax, jax.numpy as jnp
        import numpy as np
        DIM = 128
        HIDDEN = 512
        E = 8
        B, S = (2, 512)
        logits = jnp.einsum('bsd,de->bse', x, router_w) + router_b
        probs = jax.nn.softmax(logits, axis=-1)
        top1 = jnp.argmax(probs, axis=-1)
        out = jnp.zeros_like(x)
        for i in range(E):
            h = jnp.einsum('bsd,df->bsf', x, w1[i]) + b1[i]
            a, g = jnp.split(h, 2, axis=-1)
            y = jnp.einsum('bsh,hd->bsd', a * jax.nn.sigmoid(g), w2[i]) + b2[i]
            out = out + jnp.where((top1 == i)[..., None], y, 0.0)
        return out
    x = x + jnp.tanh(g_xattn[0]) * _L0_xattn_ref(ctx_2048, _layernorm(x, axis=-1), mask_BxS2_fk1, mask_BxS2_fk1, L0_xattn_W_src, L0_xattn_b_src, L0_xattn_W_tgt, L0_xattn_b_tgt, L0_xattn_W_out, L0_xattn_b_out)
    x = x + jnp.tanh(g_ffn[0]) * _L0_ffn_ref(_layernorm(x, axis=-1), L0_ffn_router_w, L0_ffn_router_b, L0_ffn_w1, L0_ffn_b1, L0_ffn_w2, L0_ffn_b2)
    return x

_drawn_inputs = setup_inputs


def setup_inputs(seed=0):
    import zlib

    import numpy as np

    out = dict(_drawn_inputs(seed))
    spreads = {'L0_xattn_b_src': (0.0, 0.1), 'L0_xattn_b_tgt': (0.0, 0.425), 'L0_xattn_b_out': (0.0, 0.1)}
    factors = {'L0_ffn_b1': 4.602, 'L0_ffn_b2': 2.704}
    for name, (base, spread) in spreads.items():
        noise = np.random.default_rng([zlib.crc32(name.encode()), seed]).standard_normal(out[name].shape)
        drawn = base * np.exp(spread * noise) if base else spread * noise
        out[name] = jnp.asarray(drawn.astype(out[name].dtype))
    for name, factor in factors.items():
        out[name] = (out[name] * factor).astype(out[name].dtype)
    return out
```

```python
import concourse.bass as bass
from concourse import mybir
from contextlib import ExitStack

B, S, D, F = 4, 256, 128, 256
H, HD = 8, 16
HP = 32
G, HG = 2, 4
P = 128
N = B * S
NT = N // P
E, HID = 8, 512
ROUTED = NT + E - 1
HC = HID // P
PAY = 2 * D + 1
EPS = 1e-5
MASKED = -2.0 ** 100
NOWHERE = 4 * N
C_ID, C_TRI, C_SUM, C_THR, C_PRI, C_TILE, C_END = 0, 128, 256, 384, 448, 456, 456 + ROUTED * E


def build(nc, x, ctxT, mask3, maskcol, wk, wq, wv, wo_x, wo_a, bqk, sel3, clear3, bv, bo, gates,
          rw, rb, w1, b1, w2, b2, consts, out):
    f32, f32r, bf16, i32 = mybir.dt.float32, mybir.dt.float32r, mybir.dt.bfloat16, mybir.dt.int32
    ALU, ACT, AX = mybir.AluOpType, mybir.ActivationFunctionType, mybir.AxisListType
    ds = bass.ds
    slots = nc.dram_tensor("slots", (ROUTED * P, PAY), f32).ap()

    with ExitStack() as ctx:
        def sb(name, shape, dt=f32):
            return ctx.enter_context(nc.sbuf_tensor(name, shape, dt))

        def sem(name):
            return ctx.enter_context(nc.semaphore(name))

        cst = sb("cst", [P, C_END])
        ident = cst[:, C_ID:C_ID + P]
        sumsel = cst[:, C_SUM:C_SUM + P]
        wq_sb = sb("wq_sb", [P, G * P])
        wox_sb = sb("wox_sb", [P, D])
        woa_sb = sb("woa_sb", [P, G, D])
        bqk_sb = sb("bqk_sb", [P, 2, G])
        mask3_sb = sb("mask3_sb", [3, N])
        sel3_sb = sb("sel3_sb", [3, 2, P])
        clear3_sb = sb("clear3_sb", [3, 2])
        maskcol_sb = sb("maskcol_sb", [P, NT])
        gates_sb = sb("gates_sb", [P, 2])
        tg = sb("tg", [P, 2])
        rw_sb = sb("rw_sb", [P, E])
        rb_sb = sb("rb_sb", [P, E])
        w1_sb = sb("w1_sb", [P, E * 2 * HID])
        w2_sb = sb("w2_sb", [P, E * HC * D])
        b2_sb = sb("b2_sb", [P, E * D])
        tri_bf = sb("tri_bf", [P, P], bf16)
        ones_bf = sb("ones_bf", [P, P], bf16)
        ones_f = sb("ones_f", [P, E])
        half_neg = sb("half_neg", [P, NT])
        stats = sb("stats", [P, NT, 6])
        mv = sb("mv", [P, NT, 2])
        veps = sb("veps", [P, NT])
        rstd = sb("rstd", [P, NT])
        stats2 = sb("stats2", [P, NT, 6])
        mv2 = sb("mv2", [P, NT, 2])
        veps2 = sb("veps2", [P, NT])
        rstd2 = sb("rstd2", [P, NT])
        xnT = sb("xnT", [P, N])
        k1 = sb("k1", [P, G, N])
        q1 = sb("q1", [P, G, N])
        k1r = sb("k1r", [P, G, N], f32r)
        q1r = sb("q1r", [P, G, N], f32r)
        vpad = sb("vpad", [P, NT, H, HP])
        negmax = sb("negmax", [P, 2, G, 2, P])
        q2 = sb("q2", [P, 2, G, S])
        qbd = sb("qbd", [P, 2, G, HG, S])
        probs = sb("probs", [P, G, 2, HG, S])
        o_sb = sb("o_sb", [P, G * S])
        rec = sb("rec", [P, G * S])
        attnT = sb("attnT", [P, G * S])
        pay = sb("pay", [P, NT, PAY])
        xn2T = sb("xn2T", [P, S])
        xb = sb("xb", [P, NT, D])

        early = sb("early", [P, E * 2 * HID])
        b1_sb = early
        taken = [0]

        def carve(*shape):
            n = 1
            for d in shape:
                n *= d
            v = early[:, taken[0]:taken[0] + n]
            taken[0] += n
            return v.rearrange("p (a b) -> p a b", a=shape[0]) if len(shape) == 2 else v

        ctx_sb, maskkq, xn, x_sb = carve(2, N), carve(2, N), carve(NT, D), carve(NT, D)
        bmv, wk_sb, wv_sb, bv_sb, bo_sb = carve(NT, D), carve(2, G * P), carve(2, D), carve(D), carve(D)
        assert taken[0] <= E * 2 * HID
        mask3b = probs[0:3, 0, 0, :, :].rearrange("p a b -> p (a b)")
        mask3t = q2[0:3, :, :, :].rearrange("p a b c -> p (a b c)")
        gsb, asb = k1[:, 0, :].rearrange("p (a b) -> p a b", a=2), k1[:, 1, :].rearrange("p (a b) -> p a b", a=2)
        sg, u = q1[:, 0, :].rearrange("p (a b) -> p a b", a=2), q1[:, 1, :].rearrange("p (a b) -> p a b", a=2)
        gT = xb[:, :, :].rearrange("p t d -> p (t d)").rearrange("p (a b) -> p a b", a=2)
        x1s = vpad[:, :, :, :].rearrange("p a b c -> p (a b c)")[:, 0:ROUTED * (D + 1)].rearrange("p (i d) -> p i d", i=ROUTED)
        lg = sb("lg", [P, 2, E])
        lmax = sb("lmax", [P, 2])
        hit = sb("hit", [P, 2, E])
        key = sb("key", [P, 2, E])
        kmax = sb("kmax", [P, 2])
        onehot = sb("onehot", [P, NT + 1, E], bf16)
        over = sb("over", [P, E, E])
        ntile = sb("ntile", [P, E])
        ends = sb("ends", [P, E])
        begins = sb("begins", [P, E])
        place = sb("place", [P, NT, E])
        placed = sb("placed", [P, NT, E])
        posf = sb("posf", [P, NT])
        pos = sb("pos", [P, NT], i32)
        past = sb("past", [P, ROUTED, E])
        npast = sb("npast", [P, ROUTED])
        expert = sb("expert", [P, ROUTED], i32)
        fill = sb("fill", [P, PAY])
        xs = sb("xs", [P, 2, D])
        xT = sb("xT", [P, 2, P])
        rs = sb("rs", [P, 2, D])
        res = sb("res", [P, 2, D])

        bank = [ctx.enter_context(nc.psum_tensor(f"bank{i}", [P, 512], f32)) for i in range(8)]

        cst_in, x_in, ctx_in, wk_in, wq_in, wv_in = map(sem, "cst_in x_in ctx_in wk_in wq_in wv_in".split())
        wo_in, small_in, mask_in, w1_in, w2_in, b1_in = map(sem, "wo_in small_in mask_in w1_in w2_in b1_in".split())
        pool_set, chain, pchain, achain = map(sem, "pool_set dve_step pool_step act_step".split())
        mask3_rdy, mask_ps, mask_rdy, var_rdy, rstd_rdy, xn_rdy = map(
            sem, "mask3_rdy mask_ps mask_rdy var_rdy rstd_rdy xn_rdy".split())
        xnT_ps, xnT_rdy, kq_ps, kq_rdy, kqr_rdy, v_ps, v_rdy, bmv_rdy, tg_rdy, xb_rdy = map(
            sem, "xnT_ps xnT_rdy kq_ps kq_rdy kqr_rdy v_ps v_rdy bmv_rdy tg_rdy xb_rdy".split())
        s1_ps, max_rdy, mt_ps, q2_rdy, qbd_rdy, s2_ps, exp_rdy, av_ps, o_rdy = map(
            sem, "s1_ps max_rdy mt_ps q2_rdy qbd_rdy s2_ps exp_rdy av_ps o_rdy".split())
        sum_ps, attn_rdy, proj_ps, var2_rdy, rstd2_rdy, xn2_rdy, xn2T_ps, xn2T_rdy, lg_ps, lg_rdy, hot_rdy = map(
            sem, "sum_ps attn_rdy proj_ps var2_rdy rstd2_rdy xn2_rdy xn2T_ps xn2T_rdy lg_ps lg_rdy hot_rdy".split())
        rank_ps, pos_rdy, expert_rdy, filled, id_rdy, sent, b2t_rdy, x1s_in = map(
            sem, "rank_ps pos_rdy expert_rdy filled id_rdy sent b2t_rdy x1s_in".split())
        xs_in = [sem("xs_in0"), sem("xs_in1")]
        out_done = [sem("out_done0"), sem("out_done1")]
        xT_ps, xT_rdy, hg_ps, ha_ps, g_rdy, a_rdy, sg_rdy, u_rdy, gT_ps, gT_rdy, y_ps, r_rdy, fin_rdy = map(
            sem, "xT_ps xT_rdy hg_ps ha_ps g_rdy a_rdy sg_rdy u_rdy gT_ps gT_rdy y_ps r_rdy fin_rdy".split())

        block = ctx.enter_context(nc.Block())
        first_steps, loop_steps, last_steps = range(-2, 3), 5, range(13, ROUTED + 1)

        def steps(eng, step):
            for s in first_steps:
                step(s, s % 2, s // 2)
            with eng.Fori(0, loop_steps) as it:
                step(it * 2 + 3, 1, it + 1)
                step(it * 2 + 4, 0, it + 2)
            for s in last_steps:
                step(s, s % 2, s // 2)

        def is_tile(i):
            return not isinstance(i, int) or 0 <= i < ROUTED

        def is_first(i):
            return isinstance(i, int) and i == 0

        def later(i, lag):
            return not isinstance(i, int) or i >= lag

        @block.sync
        def _(sp):
            sp.dma_start(x_sb[:, :, :], x.rearrange("(t p) d -> p t d", p=P)).then_inc(x_in, 16)
            sp.dma_start(wk_sb[:, :, :], wk.rearrange("(f p) o -> p f o", p=P)).then_inc(wk_in, 16)
            sp.dma_start(ctx_sb[:, :, :], ctxT.rearrange("(f p) t -> p f t", p=P)).then_inc(ctx_in, 16)
            sp.dma_start(wq_sb[:, :], wq).then_inc(wq_in, 16)
            sp.dma_start(wv_sb[:, :, :], wv.rearrange("(f p) o -> p f o", p=P)).then_inc(wv_in, 16)
            sp.dma_start(wox_sb[:, :], wo_x).then_inc(wo_in, 16)
            sp.dma_start(woa_sb[:, :, :], wo_a.rearrange("(g p) o -> p g o", p=P)).then_inc(wo_in, 16)
            sp.dma_start(w1_sb[:, :].rearrange("p (e f) -> p e f", e=E), w1.rearrange("e p f -> p e f")).then_inc(w1_in, 16)
            sp.dma_start(w2_sb[:, :].rearrange("p (e c d) -> p e c d", e=E, c=HC),
                         w2.rearrange("e (c p) d -> p e c d", p=P)).then_inc(w2_in, 16)
            sp.wait_ge(v_rdy, NT)
            sp.wait_ge(kq_rdy, 8)
            sp.wait_ge(xb_rdy, 1)
            sp.dma_start(b1_sb[:, :], b1.rearrange("e f -> (e f)").partition_broadcast(P)).then_inc(b1_in, 16)
            sp.dma_start(b2_sb[:, :], b2.rearrange("e f -> (e f)").partition_broadcast(P)).then_inc(b1_in, 16)

            sp.wait_ge(sent, 16 * NT)

            def load(i, par):
                if later(i, 2):
                    sp.wait_ge(xT_ps, i - 1)
                sp.dma_start(xs[:, par, :], slots[ds(i * P, P), 0:D]).then_inc(xs_in[par], 16)

            load(0, 0)
            load(1, 1)
            sp.dma_start(x1s[:, :, :], slots[:, D:PAY].rearrange("(i p) d -> p i d", p=P)).then_inc(x1s_in, 16)

            def step(s, par, half):
                if is_tile(s + 2) and later(s, 0):
                    load(s + 2, par)
            steps(sp, step)
            for par in range(2):
                sp.wait_ge(out_done[par], 16 * ((ROUTED + 1 - par) // 2))

        @block.gpsimd
        def _(pool):
            nc.gpsimd.memset(half_neg[:, :], -0.5).then_inc(pool_set, 1)
            nc.gpsimd.memset(negmax[:, :, :, :, :], 0.0).then_inc(pool_set, 1)
            nc.gpsimd.memset(vpad[:, :, :, HD + 1:HP], 0.0).then_inc(pool_set, 1)
            nc.gpsimd.memset(vpad[:, :, :, HD:HD + 1], 1.0).then_inc(pool_set, 1)
            nc.gpsimd.memset(qbd[:, :, :, :, :], 0.0).then_inc(pool_set, 1)
            nc.gpsimd.memset(ones_bf[:, :], 1.0).then_inc(pool_set, 1)
            nc.gpsimd.memset(ones_f[:, :], 1.0).then_inc(pool_set, 1)
            nc.gpsimd.memset(onehot[:, NT, :], 0.0).then_inc(pool_set, 1)
            nc.gpsimd.memset(fill[:, 0:2 * D], 0.0).then_inc(pool_set, 1)
            nc.gpsimd.iota(fill[:, 2 * D:PAY].bitcast(i32), pattern=[[0, 1]], base=NOWHERE,
                           channel_multiplier=0).then_inc(pool_set, 1)
            nc.gpsimd.iota(pay[:, :, 2 * D:PAY].bitcast(i32), pattern=[[P, NT], [0, 1]], base=0,
                           channel_multiplier=1).then_inc(id_rdy, 1)

            def inverse_roots(n0, n1, var, tmp, root, ready, value, done):
                pool.wait_ge(ready, value)
                nc.gpsimd.tensor_scalar(tmp[:, n0:n1], var[:, n0:n1, 1], EPS, None, ALU.add).then_inc(pchain, 1)
                pchained[0] += 1
                pool.wait_ge(pchain, pchained[0])
                nc.gpsimd.tensor_tensor(root[:, n0:n1], tmp[:, n0:n1], half_neg[:, n0:n1], ALU.pow).then_inc(done, 1)
            pchained = [0]
            pool.wait_ge(pool_set, 10)
            inverse_roots(0, NT, mv, veps, rstd, var_rdy, 1, rstd_rdy)
            pool.wait_ge(rstd_rdy, 1)
            pool.dma_start(slots.rearrange("(i p) d -> p i d", p=P),
                           fill[:, :].unsqueeze(1).broadcast_to([P, ROUTED, PAY])).then_inc(filled, 16)
            pool.wait_ge(small_in, 16 * 7)
            for t in range(NT):
                nc.gpsimd.tensor_scalar(bmv[:, t, :], bv_sb, maskcol_sb[:, t:t + 1], None, ALU.mult).then_inc(bmv_rdy, 1)
            pool.wait_ge(cst_in, 16)
            nc.gpsimd.tensor_copy(tri_bf[:, :], cst[:, C_TRI:C_TRI + P]).then_inc(pool_set, 1)

            for b in range(B + 1):
                par = b % 2
                if b < B:
                    pool.wait_ge(q2_rdy, b + 1)
                    pool.wait_ge(pool_set, 11)
                    if b >= 2:
                        pool.wait_ge(rstd2_rdy, b - 1)
                    if b >= 2:
                        pool.wait_ge(s2_ps, 8 * (b - 1))
                    for j in range(HG):
                        nc.gpsimd.tensor_copy(qbd[HP * j:HP * (j + 1), par, :, j, :],
                                              q2[HP * j:HP * (j + 1), par, :, :]).then_inc(qbd_rdy, 1)
                pool.wait_ge(qbd_rdy, HG * min(b + 1, B))
                if b >= 1:
                    inverse_roots(2 * b - 2, 2 * b, mv2, veps2, rstd2, var2_rdy, b, rstd2_rdy)
            pool.wait_ge(b1_in, 32)
            pool.wait_ge(tg_rdy, 1)
            nc.gpsimd.tensor_scalar(b2_sb[:, :], b2_sb[:, :], tg[:, 1:2], None, ALU.mult).then_inc(b2t_rdy, 1)

            pool.wait_ge(filled, 16)
            pool.wait_ge(id_rdy, 1)
            pool.wait_ge(pos_rdy, 1)
            for t in range(NT):
                pool.indirect_dma_start(out=slots, out_offset=bass.IndirectOffsetOnAxis(ap=pos[:, t:t + 1], axis=0),
                                        in_=pay[:, t, :], in_offset=None).then_inc(sent, 16)

            def step(s, par, half):
                i = s + 1
                if is_tile(i):
                    if is_first(i):
                        pool.wait_ge(x1s_in, 16)
                        pool.wait_ge(b2t_rdy, 1)
                        pool.wait_ge(expert_rdy, 1)
                    e = pool.value_load(expert[0:1, ds(i, 1)], min_val=0, max_val=E - 1)
                    if later(i, 2):
                        pool.wait_ge(fin_rdy, i - 1)
                    nc.gpsimd.tensor_tensor(rs[:, 1 - par, :], x1s[:, i, 0:D], b2_sb[:, ds(e * D, D)], ALU.add).then_inc(r_rdy, 1)
                i = s - 1
                if is_tile(i):
                    pool.wait_ge(fin_rdy, i + 1)
                    pool.indirect_dma_start(out=out, out_offset=bass.IndirectOffsetOnAxis(ap=x1s[:, i, D:D + 1].bitcast(i32), axis=0),
                                            in_=res[:, 1 - par, :], in_offset=None, bounds_check=N - 1,
                                            oob_is_err=False).then_inc(out_done[1 - par], 16)
            for s in range(-2, ROUTED + 1):
                step(s, s % 2, s // 2)

        @block.scalar
        def _(act):
            act.dma_start(mask3_sb[:, :], mask3).then_inc(mask_in, 16)
            act.dma_start(clear3_sb[:, :], clear3).then_inc(mask_in, 16)
            act.dma_start(sel3_sb[:, :, :], sel3.rearrange("a (s p) -> a s p", s=2)).then_inc(mask_in, 16)
            act.dma_start(cst[:, :], consts).then_inc(cst_in, 16)
            act.dma_start(bqk_sb[:, :, :], bqk.rearrange("p (s g) -> p s g", s=2)).then_inc(small_in, 16)
            act.dma_start(gates_sb[:, :], gates.partition_broadcast(P)).then_inc(small_in, 16)
            act.dma_start(maskcol_sb[:, :], maskcol).then_inc(small_in, 16)
            act.dma_start(bv_sb, bv.partition_broadcast(P)).then_inc(small_in, 16)
            act.dma_start(bo_sb, bo.partition_broadcast(P)).then_inc(small_in, 16)
            act.dma_start(rw_sb[:, :], rw).then_inc(small_in, 16)
            act.dma_start(rb_sb[:, :], rb.partition_broadcast(P)).then_inc(small_in, 16)

            for side in range(2):
                act.wait_ge(mask_ps, side + 1)
                for half in range(2):
                    nc.scalar.activation(maskkq[:, side, half * 512:half * 512 + 512], bank[4 + 2 * side + half][:, :],
                                         ACT.Copy).then_inc(mask_rdy, 1)
            for half in range(2):
                act.wait_ge(xnT_ps, half + 1)
                nc.scalar.activation(xnT[:, half * 512:half * 512 + 512], bank[half][:, :], ACT.Copy).then_inc(xnT_rdy, 1)
            act.wait_ge(small_in, 16 * 7)
            nc.scalar.activation(tg[:, :], gates_sb[:, :], ACT.Tanh).then_inc(tg_rdy, 1)
            for n in range(8):
                src, dst = ((k1, k1r), (q1, q1r))[n // 4]
                g, half = n % 4 // 2, n % 2
                act.wait_ge(kq_rdy, n + 1)
                nc.scalar.activation(dst[:, g, half * 512:half * 512 + 512], src[:, g, half * 512:half * 512 + 512],
                                     ACT.Copy).then_inc(kqr_rdy, 1)

            for b in range(B + 1):
                if b < B:
                    for g in range(G):
                        if b >= 1:
                            act.wait_ge(av_ps, 2 * (b - 1) + g + 1)
                        for n in range(4):
                            st, hf = n // 2, n % 2
                            m = 8 * b + 4 * g + n
                            act.wait_ge(s2_ps, m + 1)
                            nc.scalar.activation(probs[:, g, st, 2 * hf:2 * hf + 2, :].rearrange("p j t -> p (j t)"),
                                                 bank[4 + m % 2][:, :], ACT.Exp, scale=HD ** -0.5).then_inc(exp_rdy, 1)
                    act.wait_ge(av_ps, 2 * b + 2)
                    if b >= 1:
                        act.wait_ge(attn_rdy, b)
                    nc.scalar.activation(o_sb[:, :], bank[6][:, :], ACT.Copy).then_inc(o_rdy, 1)
                if b >= 1:
                    act.wait_ge(xn2T_ps, b)
                    nc.scalar.activation(xn2T[:, :], bank[7][:, 256:512], ACT.Copy).then_inc(xn2T_rdy, 1)

            def step(s, par, half):
                i = s + 1
                if is_tile(i):
                    act.wait_ge(g_rdy, i + 1)
                    if later(i, 2):
                        act.wait_ge(u_rdy, i - 1)
                    nc.scalar.activation(sg[:, 1 - par, :], gsb[:, 1 - par, :], ACT.Sigmoid).then_inc(sg_rdy, 1)
                i = s + 2
                if is_tile(i):
                    act.wait_ge(xT_ps, i + 1)
                    if later(i, 2):
                        act.wait_ge(ha_ps, i - 1)
                    nc.scalar.activation(xT[:, par, :], bank[4][:, 0:P], ACT.Copy).then_inc(xT_rdy, 1)
                i = s
                if is_tile(i):
                    act.wait_ge(gT_ps, i + 1)
                    if later(i, 2):
                        act.wait_ge(y_ps, i - 1)
                    nc.scalar.activation(gT[:, par, :], bank[5][:, :], ACT.Copy).then_inc(gT_rdy, 1)
            steps(act, step)

        @block.vector
        def _(dve):
            linked = [0]

            def link(ins):
                ins.then_inc(chain, 1)
                linked[0] += 1
                dve.wait_ge(chain, linked[0])

            dve.wait_ge(mask_in, 48)
            link(nc.vector.tensor_scalar(mask3t[:, :], mask3_sb[:, :], 0.0, clear3_sb[:, 0:1], ALU.is_equal, ALU.mult))
            nc.vector.scalar_tensor_tensor(mask3b[:, :], mask3_sb[:, :], clear3_sb[:, 1:2], mask3t[:, :],
                                           ALU.mult, ALU.add).then_inc(mask3_rdy, 1)

            dve.wait_ge(x_in, 16)
            for t in range(NT):
                last = nc.vector.bn_stats(stats[:, t, :], x_sb[:, t, :])
                if t < NT - 1:
                    last.then_inc(chain, 1)
                    linked[0] += 1
            link(last)
            for t in range(NT):
                last = nc.vector.bn_aggr(mv[:, t, :], stats[:, t, :])
            last.then_inc(var_rdy, 1)
            dve.wait_ge(var_rdy, 1)
            dve.wait_ge(rstd_rdy, 1)
            for t in range(NT):
                nc.vector.tensor_scalar(xn[:, t, :], x_sb[:, t, :], mv[:, t, 0:1], rstd[:, t:t + 1],
                                        ALU.subtract, ALU.mult).then_inc(xn_rdy, 1)
            dve.wait_ge(small_in, 16 * 7)
            for n in range(8):
                side, g, half = n // 4, n % 4 // 2, n % 2
                dve.wait_ge(kq_ps, n + 1)
                dve.wait_ge(mask_rdy, 2 * side + half + 1)
                nc.vector.scalar_tensor_tensor((k1, q1)[side][:, g, half * 512:half * 512 + 512],
                                               bank[KQ_BANK[n]][:, :], bqk_sb[:, 1 - side, g:g + 1],
                                               maskkq[:, side, half * 512:half * 512 + 512],
                                               ALU.add, ALU.mult).then_inc(kq_rdy, 1)
            dve.wait_ge(tg_rdy, 1)
            nc.vector.scalar_tensor_tensor(xb[:, :, :], bo_sb.unsqueeze(1).broadcast_to([P, NT, D]), tg[:, 0:1],
                                           x_sb[:, :, :], ALU.mult, ALU.add).then_inc(xb_rdy, 1)
            dve.wait_ge(bmv_rdy, NT)
            dve.wait_ge(pool_set, 10)
            for t in range(NT):
                dve.wait_ge(v_ps, t // 4 + 1)
                nc.vector.scalar_tensor_tensor(vpad[:, t, :, 0:HD],
                                               bank[2 + t // 4][:, t % 4 * D:t % 4 * D + D].rearrange("p (h d) -> p h d", h=H),
                                               maskcol_sb[:, t:t + 1], bmv[:, t, :].rearrange("p (h d) -> p h d", h=H),
                                               ALU.mult, ALU.add).then_inc(v_rdy, 1)

            def maxima(b, g):
                if b >= 2 and g == 0:
                    dve.wait_ge(mt_ps, b - 1)
                for j in range(HG):
                    dve.wait_ge(s1_ps, (2 * b + g) * HG + j + 1)
                    nc.vector.tensor_reduce(negmax[:, b % 2, g, :, HP * j + HD], bank[j][:, :].rearrange("p (t s) -> p t s", t=2),
                                            AX.X, ALU.max, negate=True).then_inc(max_rdy, 1)

            def normalise(b):
                dve.wait_ge(sum_ps, b + 1)
                link(nc.vector.reciprocal(rec[:, :], bank[7][:, :]))
                if b >= 1:
                    dve.wait_ge(proj_ps, b)
                nc.vector.tensor_tensor(attnT[:, :], o_sb[:, :], rec[:, :], ALU.mult).then_inc(attn_rdy, 1)

            def residual(b):
                dve.wait_ge(proj_ps, b + 1)
                dve.wait_ge(xb_rdy, 1)
                link(nc.vector.scalar_tensor_tensor(pay[:, 2 * b:2 * b + 2, D:2 * D],
                                                    bank[7][:, 0:2 * D].rearrange("p (t d) -> p t d", t=2), tg[:, 0:1],
                                                    xb[:, 2 * b:2 * b + 2, :], ALU.mult, ALU.add))
                nc.vector.bn_stats(stats2[:, 2 * b, :], pay[:, 2 * b, D:2 * D]).then_inc(chain, 1)
                linked[0] += 1
                link(nc.vector.bn_stats(stats2[:, 2 * b + 1, :], pay[:, 2 * b + 1, D:2 * D]))
                nc.vector.bn_aggr(mv2[:, 2 * b, :], stats2[:, 2 * b, :])
                nc.vector.bn_aggr(mv2[:, 2 * b + 1, :], stats2[:, 2 * b + 1, :]).then_inc(var2_rdy, 1)

            def second_norm(b):
                dve.wait_ge(var2_rdy, b + 1)
                dve.wait_ge(rstd2_rdy, b + 1)
                for t in range(2 * b, 2 * b + 2):
                    nc.vector.tensor_scalar(pay[:, t, 0:D], pay[:, t, D:2 * D], mv2[:, t, 0:1], rstd2[:, t:t + 1],
                                            ALU.subtract, ALU.mult).then_inc(xn2_rdy, 1)

            def route(b):
                dve.wait_ge(lg_ps, b + 1)
                nc.vector.tensor_tensor(lg[:, :, :], bank[7][:, 0:2 * E].rearrange("p (t e) -> p t e", t=2),
                                        rb_sb[:, :].unsqueeze(1).broadcast_to([P, 2, E]), ALU.add).then_inc(lg_rdy, 1)
                dve.wait_ge(lg_rdy, b + 1)
                link(nc.vector.tensor_reduce(lmax[:, :], lg[:, :, :], AX.X, ALU.max))
                link(nc.vector.tensor_tensor(hit[:, :, :], lg[:, :, :], lmax[:, :].unsqueeze(2).broadcast_to([P, 2, E]), ALU.is_equal))
                link(nc.vector.tensor_tensor(key[:, :, :], hit[:, :, :],
                                             cst[:, C_PRI:C_PRI + E].unsqueeze(1).broadcast_to([P, 2, E]), ALU.mult))
                link(nc.vector.tensor_reduce(kmax[:, :], key[:, :, :], AX.X, ALU.max))
                nc.vector.tensor_tensor(onehot[:, 2 * b:2 * b + 2, :], key[:, :, :],
                                        kmax[:, :].unsqueeze(2).broadcast_to([P, 2, E]), ALU.is_equal).then_inc(hot_rdy, 1)

            for b in range(2):
                for g in range(G):
                    maxima(b, g)
            dve.wait_ge(cst_in, 16)
            for b in range(B + 1):
                if b < B:
                    dve.wait_ge(mt_ps, b + 1)
                    if b >= 2:
                        dve.wait_ge(qbd_rdy, HG * (b - 1))
                    nc.vector.tensor_tensor(q2[:, b % 2, :, :], q1[:, :, b * S:(b + 1) * S],
                                            bank[7][:, :].rearrange("p (g t) -> p g t", g=G), ALU.add).then_inc(q2_rdy, 1)
                if b >= 1:
                    normalise(b - 1)
                    residual(b - 1)
                if b + 2 < B:
                    maxima(b + 2, 0)
                if b >= 1:
                    second_norm(b - 1)
                if b + 2 < B:
                    maxima(b + 2, 1)
                if b >= 1:
                    route(b - 1)

            dve.wait_ge(rank_ps, 1)
            total = bank[0][:, NT * E:(NT + 1) * E]
            link(nc.vector.tensor_tensor(over[:, :, :], total.unsqueeze(2).broadcast_to([P, E, E]),
                                         cst[:, C_THR:C_THR + E * E].rearrange("p (e k) -> p e k", e=E), ALU.is_gt))
            link(nc.vector.tensor_reduce(ntile[:, :], over[:, :, :], AX.X, ALU.add))
            link(nc.vector.tensor_tensor_scan(ends[:, :], ones_f[:, :], ntile[:, :], 0.0, ALU.mult, ALU.add))
            link(nc.vector.tensor_tensor(begins[:, :], ends[:, :], ntile[:, :], ALU.subtract))
            link(nc.vector.scalar_tensor_tensor(place[:, :, :], begins[:, :].unsqueeze(1).broadcast_to([P, NT, E]), float(P),
                                                bank[0][:, 0:NT * E].rearrange("p (t e) -> p t e", t=NT), ALU.mult, ALU.add))
            link(nc.vector.tensor_tensor(placed[:, :, :], place[:, :, :], onehot[:, 0:NT, :], ALU.mult))
            link(nc.vector.tensor_reduce(posf[:, :], placed[:, :, :], AX.X, ALU.add))
            nc.vector.tensor_copy(pos[:, :], posf[:, :]).then_inc(pos_rdy, 1)
            link(nc.vector.tensor_tensor(past[:, :, :], ends[:, :].unsqueeze(1).broadcast_to([P, ROUTED, E]),
                                         cst[:, C_TILE:C_END].rearrange("p (i e) -> p i e", i=ROUTED), ALU.is_le))
            link(nc.vector.tensor_reduce(npast[:, :], past[:, :, :], AX.X, ALU.add))
            nc.vector.tensor_scalar(expert[:, :], npast[:, :], float(E - 1), None, ALU.min).then_inc(expert_rdy, 1)
            dve.wait_ge(expert_rdy, 1)

            def step(s, par, half):
                i = s + 1
                if is_tile(i):
                    if is_first(i):
                        dve.wait_ge(b1_in, 32)
                    e = dve.value_load(expert[0:1, ds(i, 1)], min_val=0, max_val=E - 1)
                    dve.wait_ge(hg_ps, i + 1)
                    nc.vector.tensor_tensor(gsb[:, 1 - par, :], bank[4 - 2 * par - 2][:, :],
                                            b1_sb[:, ds(e * (2 * HID) + HID, HID)], ALU.add).then_inc(g_rdy, 1)
                    dve.wait_ge(ha_ps, i + 1)
                    nc.vector.tensor_tensor(asb[:, 1 - par, :], bank[4 - 2 * par - 1][:, :],
                                            b1_sb[:, ds(e * (2 * HID), HID)], ALU.add).then_inc(a_rdy, 1)
                    dve.wait_ge(a_rdy, i + 1)
                    dve.wait_ge(sg_rdy, i + 1)
                    if later(i, 2):
                        dve.wait_ge(gT_ps, i - 1)
                    nc.vector.tensor_tensor(u[:, 1 - par, :], asb[:, 1 - par, :], sg[:, 1 - par, :], ALU.mult).then_inc(u_rdy, 1)
                i = s - 1
                if is_tile(i):
                    dve.wait_ge(y_ps, i + 1)
                    dve.wait_ge(r_rdy, i + 1)
                    if later(i, 2):
                        dve.wait_ge(out_done[1 - par], 16 * (i // 2 if isinstance(i, int) else half - (1 - par)))
                    nc.vector.scalar_tensor_tensor(res[:, 1 - par, :], bank[6 + 1 - par][:, 0:D], tg[:, 1:2],
                                                   rs[:, 1 - par, :], ALU.mult, ALU.add).then_inc(fin_rdy, 1)
            steps(dve, step)

        @block.tensor
        def _(pe):
            pe.wait_ge(mask3_rdy, 1)
            for side in range(2):
                for half in range(2):
                    mm = nc.tensor.matmul(bank[4 + 2 * side + half][:, :], sel3_sb[:, side, :],
                                          mask3b[:, half * 512:half * 512 + 512], start=True, stop=True)
                mm.then_inc(mask_ps, 1)

            def project(n):
                side, g, half = n // 4, n % 4 // 2, n % 2
                cols = slice(half * 512, half * 512 + 512)
                if side == 0:
                    for f in range(2):
                        mm = nc.tensor.matmul(bank[KQ_BANK[n]][:, :], wk_sb[:, f, g * P:(g + 1) * P], ctx_sb[:, f, cols],
                                              start=f == 0, stop=f == 1)
                else:
                    mm = nc.tensor.matmul(bank[KQ_BANK[n]][:, :], wq_sb[:, g * P:(g + 1) * P], xnT[:, cols], start=True, stop=True)
                mm.then_inc(kq_ps, 1)

            pe.wait_ge(wk_in, 16)
            pe.wait_ge(ctx_in, 16)
            project(0)
            project(1)
            pe.wait_ge(cst_in, 16)
            for t in range(NT):
                pe.wait_ge(xn_rdy, t + 1)
                mm = nc.tensor.transpose(bank[t // 4][:, t % 4 * P:t % 4 * P + P], xn[:, t, :], ident)
                if t % 4 == 3:
                    mm.then_inc(xnT_ps, 1)
            pe.wait_ge(mask_rdy, 2)
            project(2)
            project(3)
            pe.wait_ge(wq_in, 16)
            pe.wait_ge(mask_rdy, 4)
            pe.wait_ge(xnT_rdy, 2)
            for n in range(4, 8):
                project(n)
            pe.wait_ge(wv_in, 16)
            pe.wait_ge(kq_rdy, 2)
            for t in range(NT):
                for f in range(2):
                    mm = nc.tensor.matmul(bank[2 + t // 4][:, t % 4 * D:t % 4 * D + D], ctx_sb[:, f, t * P:(t + 1) * P],
                                          wv_sb[:, f, :], start=f == 0, stop=f == 1)
                if t % 4 == 3:
                    mm.then_inc(v_ps, 1)

            def scores_for_max(b):
                for g in range(G):
                    n = 2 * b + g
                    for tt in range(2):
                        for j in range(HG):
                            if tt == 0 and n >= 1:
                                pe.wait_ge(max_rdy, (n - 1) * HG + j + 1)
                            q0 = b * S + tt * P
                            mm = nc.tensor.matmul(bank[j][:, tt * S:(tt + 1) * S], q1r[HP * j:HP * (j + 1), g, q0:q0 + P],
                                                  k1r[HP * j:HP * (j + 1), g, b * S:(b + 1) * S], start=True, stop=True)
                            if tt == 1:
                                mm.then_inc(s1_ps, 1)

            def transpose_max(b):
                pe.wait_ge(max_rdy, 2 * HG * (b + 1))
                if b >= 2:
                    pe.wait_ge(lg_rdy, b - 1)
                for g in range(G):
                    for tt in range(2):
                        c = (2 * g + tt) * P
                        mm = nc.tensor.transpose(bank[7][:, c:c + P], negmax[:, b % 2, g, tt, :], ident)
                mm.then_inc(mt_ps, 1)

            def scores(b, g):
                pe.wait_ge(qbd_rdy, HG * (b + 1))
                for n in range(4):
                    st, hf = n // 2, n % 2
                    m = 8 * b + 4 * g + n
                    if m >= 2:
                        pe.wait_ge(exp_rdy, m - 1)
                    k0 = b * S + st * P
                    nc.tensor.matmul(bank[4 + m % 2][:, :], k1[:, g, k0:k0 + P],
                                     qbd[:, b % 2, g, 2 * hf:2 * hf + 2, :].rearrange("p j t -> p (j t)"),
                                     start=True, stop=True).then_inc(s2_ps, 1)

            def values(b, g):
                if g == 0 and b >= 1:
                    pe.wait_ge(o_rdy, b)
                for st in range(2):
                    pe.wait_ge(exp_rdy, 8 * b + 4 * g + 2 * st + 2)
                    for j in range(HG):
                        mm = nc.tensor.matmul(bank[6][HP * j:HP * (j + 1), g * S:(g + 1) * S], vpad[:, 2 * b + st, HG * g + j, :],
                                              probs[:, g, st, j, :], start=st == 0, stop=st == 1)
                mm.then_inc(av_ps, 1)

            def spread_sums(b):
                pe.wait_ge(o_rdy, b + 1)
                nc.tensor.matmul(bank[7][:, :], sumsel, o_sb[:, :], start=True, stop=True).then_inc(sum_ps, 1)

            def output_projection(b):
                pe.wait_ge(attn_rdy, b + 1)
                for tt in range(2):
                    t0 = b * S + tt * P
                    o = bank[7][:, tt * D:(tt + 1) * D]
                    nc.tensor.matmul(o, xnT[:, t0:t0 + P], wox_sb[:, :], start=True, stop=False)
                    for g in range(G):
                        mm = nc.tensor.matmul(o, attnT[:, g * S + tt * P:g * S + tt * P + P], woa_sb[:, g, :],
                                              start=False, stop=g == G - 1)
                mm.then_inc(proj_ps, 1)

            def router(b):
                pe.wait_ge(xn2_rdy, 2 * (b + 1))
                for tt in range(2):
                    mm = nc.tensor.transpose(bank[7][:, 256 + tt * P:256 + tt * P + P], pay[:, 2 * b + tt, 0:D], ident)
                mm.then_inc(xn2T_ps, 1)
                pe.wait_ge(xn2T_rdy, b + 1)
                for tt in range(2):
                    mm = nc.tensor.matmul(bank[7][:, tt * E:(tt + 1) * E], xn2T[:, tt * P:(tt + 1) * P], rw_sb[:, :],
                                          start=True, stop=True)
                mm.then_inc(lg_ps, 1)

            pe.wait_ge(kq_rdy, 8)
            pe.wait_ge(v_rdy, NT)
            pe.wait_ge(kqr_rdy, 8)
            scores_for_max(0)
            scores_for_max(1)
            pe.wait_ge(wo_in, 32)
            for b in range(B + 1):
                if b < B:
                    transpose_max(b)
                    scores(b, 0)
                    values(b, 0)
                if b >= 1:
                    pe.wait_ge(q2_rdy, min(b + 1, B))
                    if b == B:
                        pe.wait_ge(lg_rdy, B - 1)
                    spread_sums(b - 1)
                if b < B:
                    scores(b, 1)
                    values(b, 1)
                if b >= 1:
                    output_projection(b - 1)
                if b + 2 < B:
                    scores_for_max(b + 2)
                if b >= 1:
                    router(b - 1)

            pe.wait_ge(pool_set, 11)
            pe.wait_ge(hot_rdy, B)
            ranks = bank[0][:, 0:(NT + 1) * E].rearrange("p (t e) -> p t e", e=E)
            nc.tensor.matmul(ranks, tri_bf[:, :], onehot[:, :, :], start=True, stop=False)
            for t in range(NT):
                mm = nc.tensor.matmul(ranks[:, t + 1:NT + 1, :], ones_bf[:, :],
                                      onehot[:, t:t + 1, :].broadcast_to([P, NT - t, E]), start=False, stop=t == NT - 1)
            mm.then_inc(rank_ps, 1)

            def step(s, par, half):
                i = s + 1
                if is_tile(i):
                    if is_first(i):
                        pe.wait_ge(w1_in, 16)
                        pe.wait_ge(expert_rdy, 1)
                    e = pe.value_load(expert[0:1, ds(i, 1)], min_val=0, max_val=E - 1)
                    pe.wait_ge(xT_rdy, i + 1)
                    if later(i, 2):
                        pe.wait_ge(a_rdy, i - 1)
                    nc.tensor.matmul(bank[2 * (1 - par)][:, :], xT[:, 1 - par, :], w1_sb[:, ds(e * (2 * HID) + HID, HID)],
                                     start=True, stop=True).then_inc(hg_ps, 1)
                    nc.tensor.matmul(bank[2 * (1 - par) + 1][:, :], xT[:, 1 - par, :], w1_sb[:, ds(e * (2 * HID), HID)],
                                     start=True, stop=True).then_inc(ha_ps, 1)
                i = s + 2
                if is_tile(i):
                    pe.wait_ge(xs_in[par], 16 * (half + 2))
                    if later(i, 1):
                        pe.wait_ge(xT_rdy, i)
                    nc.tensor.transpose(bank[4][:, 0:P], xs[:, par, :], ident).then_inc(xT_ps, 1)
                i = s
                if is_tile(i):
                    pe.wait_ge(u_rdy, i + 1)
                    if later(i, 1):
                        pe.wait_ge(gT_rdy, i)
                    for c in range(HC):
                        mm = nc.tensor.transpose(bank[5][:, c * P:(c + 1) * P], u[:, par, c * P:(c + 1) * P], ident)
                    mm.then_inc(gT_ps, 1)
                i = s - 1
                if is_tile(i):
                    if is_first(i):
                        pe.wait_ge(w2_in, 16)
                    e = pe.value_load(expert[0:1, ds(i, 1)], min_val=0, max_val=E - 1)
                    pe.wait_ge(gT_rdy, i + 1)
                    if later(i, 2):
                        pe.wait_ge(fin_rdy, i - 1)
                    for c in range(HC):
                        mm = nc.tensor.matmul(bank[6 + 1 - par][:, 0:D], gT[:, 1 - par, c * P:(c + 1) * P],
                                              w2_sb[:, ds(e * (HC * D) + c * D, D)], start=c == 0, stop=c == HC - 1)
                    mm.then_inc(y_ps, 1)
            steps(pe, step)


KQ_BANK = [2, 3, 4, 5, 6, 7, 0, 1]


def pad_heads(a):
    import numpy as np
    a = a.reshape(a.shape[:-1] + (H, HD))
    return np.concatenate([a, np.zeros(a.shape[:-1] + (HP - HD,), a.dtype)], -1).reshape(a.shape[:-2] + (H * HP,))


def shape_constants():
    import numpy as np
    f = np.float32
    c = np.zeros((P, C_END), f)
    c[:, C_ID:C_ID + P] = np.eye(P, dtype=f)
    c[:, C_TRI:C_TRI + P] = np.triu(np.ones((P, P), f), 1)
    head = np.arange(P) // HP
    c[head[:] * HP + HD, C_SUM + np.arange(P)] = 1
    c[:, C_THR:C_THR + E * E] = np.tile(np.arange(E) * P, E)
    c[:, C_PRI:C_PRI + E] = E - np.arange(E)
    c[:, C_TILE:C_END] = np.repeat(np.arange(ROUTED), E)
    row = np.arange(P) % HP
    sel3 = np.zeros((3, 2, P), f)
    sel3[0, :, row < HD] = 1
    sel3[2, 0, row == HD] = 1
    sel3[1, 0, row == HD + 1] = 1
    sel3[2, 1, row == HD + 1] = 1
    clear3 = np.array([[0, 1], [MASKED, 0], [0, 1]], f)
    return c, sel3.reshape(3, 2 * P), clear3


def kernel(x, ctx_2048, mask_BxS2_fk1, g_xattn, g_ffn, L0_xattn_W_src, L0_xattn_b_src, L0_xattn_W_tgt, L0_xattn_b_tgt,
           L0_xattn_W_out, L0_xattn_b_out, L0_ffn_router_w, L0_ffn_router_b, L0_ffn_w1, L0_ffn_b1, L0_ffn_w2, L0_ffn_b2):
    import numpy as np
    import concourse.bacc as bacc
    from concourse.bass_utils import run_bass_kernel_spmd as run

    a = np.asarray
    consts, sel3, clear3 = shape_constants()
    mask = a(mask_BxS2_fk1).reshape(1, N)
    w_src, b_src, w_out = a(L0_xattn_W_src), a(L0_xattn_b_src), a(L0_xattn_W_out)
    row = np.arange(P) % HP
    bq = pad_heads(a(L0_xattn_b_tgt)).reshape(G, P).T.copy()
    bk = pad_heads(b_src[:D]).reshape(G, P).T.copy()
    bq[row == HD + 1] = 1
    bk[(row == HD) | (row == HD + 1)] = 1
    arrays = {
        "x": a(x).reshape(N, D),
        "ctxT": a(ctx_2048).reshape(N, F).T,
        "mask3": np.concatenate([mask, mask, np.ones_like(mask)]),
        "maskcol": mask.reshape(NT, P).T,
        "wk": pad_heads(w_src[:D].T),
        "wq": pad_heads(a(L0_xattn_W_tgt).T),
        "wv": w_src[D:].T,
        "wo_x": w_out[:, :D].T,
        "wo_a": pad_heads(w_out[:, D:]).T,
        "bqk": np.concatenate([bq, bk], 1),
        "sel3": sel3, "clear3": clear3,
        "bv": b_src[D:], "bo": a(L0_xattn_b_out),
        "gates": np.concatenate([a(g_xattn), a(g_ffn)]),
        "rw": a(L0_ffn_router_w), "rb": a(L0_ffn_router_b),
        "w1": a(L0_ffn_w1), "b1": a(L0_ffn_b1), "w2": a(L0_ffn_w2), "b2": a(L0_ffn_b2),
        "consts": consts,
    }
    nc = bacc.Bacc("TRN2", target_bir_lowering=False, num_devices=1)
    arrays = {f"in_{k}": np.ascontiguousarray(v) for k, v in arrays.items()}
    args = [nc.dram_tensor(k, v.shape, mybir.dt.from_np(v.dtype), kind="ExternalInput").ap() for k, v in arrays.items()]
    out = nc.dram_tensor("out_0", (N, D), mybir.dt.float32, kind="ExternalOutput").ap()
    build(nc, *args, out)
    r = run(nc, [arrays], core_ids=[0])
    return np.asarray(r.results[0]["out_0"]).reshape(B, S, D)
```

```python
import concourse.bass as bass
from concourse import mybir
from contextlib import ExitStack

B, S, D, F = 4, 256, 128, 256
H, HD = 8, 16
HP = 32
G, HG = 2, 4
P = 128
N = B * S
NT = N // P
E, HID = 8, 512
ROUTED = NT + E - 1
HC = HID // P
PAY = D + 1
EPS = 1e-5
MASKED = -2.0 ** 100
NOWHERE = 4 * N
A_WK, A_BQK, A_MASK, A_GATES, A_END = 0, 512, 516, 524, 526
B_ID, B_WQ, B_RW, B_RB, B_TRI, B_THR, B_PRI, B_ROW, B_TILE, B_TROW = 0, 128, 384, 392, 400, 528, 592, 600, 616, 736
B_END = 751
C_WV, C_WOX, C_WOA, C_BV, C_BO, C_END = 0, 256, 384, 512, 640, 768
assert B_TROW + ROUTED == B_END


def build(nc, x, ctxT, mask3, pack_a, pack_b, pack_c, w1, b1, w2, b2, out):
    f32, f32r, bf16, i32 = mybir.dt.float32, mybir.dt.float32r, mybir.dt.bfloat16, mybir.dt.int32
    ALU, ACT, AX = mybir.AluOpType, mybir.ActivationFunctionType, mybir.AxisListType
    ds = bass.ds
    slots = nc.dram_tensor("slots", (E * N + P, PAY), f32).ap()
    x1_dram = nc.dram_tensor("x1_dram", (N, D), f32).ap()

    with ExitStack() as ctx:
        def sb(name, shape, dt=f32):
            return ctx.enter_context(nc.sbuf_tensor(name, shape, dt))

        def sem(name):
            return ctx.enter_context(nc.semaphore(name))

        b_sb = sb("b_sb", [P, B_END])
        ident = b_sb[:, B_ID:B_ID + P]
        wq_sb = b_sb[:, B_WQ:B_WQ + G * P]
        rw_sb, rb_sb = b_sb[:, B_RW:B_RW + E], b_sb[:, B_RB:B_RB + E]
        c_sb = sb("c_sb", [P, C_END])
        wv_sb = c_sb[:, C_WV:C_WV + 2 * D].rearrange("p (f d) -> p f d", f=2)
        wox_sb, woa_sb = c_sb[:, C_WOX:C_WOX + D], c_sb[:, C_WOA:C_WOA + D]
        bv_sb, bo_sb = c_sb[:, C_BV:C_BV + D], c_sb[:, C_BO:C_BO + D]
        m_sb = sb("m_sb", [3, N + 2 * P + 2])
        mask3_sb, clear3_sb = m_sb[:, 0:N], m_sb[:, N + 2 * P:N + 2 * P + 2]
        sel3_sb = m_sb[:, N:N + 2 * P].rearrange("a (s p) -> a s p", s=2)
        maskcol_sb = sb("maskcol_sb", [P, NT])
        tg = sb("tg", [P, 2])
        warm = sb("warm", [1, 2])
        w1_sb = sb("w1_sb", [P, E * 2 * HID])
        w2_sb = sb("w2_sb", [P, E * HC * D])
        b2_sb = sb("b2_sb", [P, E * D])
        tri_bf = sb("tri_bf", [P, P], bf16)
        ones_bf = sb("ones_bf", [P, P], bf16)
        ones_f = sb("ones_f", [P, E])
        half_neg = sb("half_neg", [P, NT])
        stats = sb("stats", [P, NT, 6])
        mv = sb("mv", [P, NT, 2])
        veps = sb("veps", [P, NT])
        rstd = sb("rstd", [P, NT])
        stats2 = sb("stats2", [P, NT, 6])
        mv2 = sb("mv2", [P, NT, 2])
        veps2 = sb("veps2", [P, NT])
        rstd2 = sb("rstd2", [P, NT])
        xnT = sb("xnT", [P, N])
        k1 = sb("k1", [P, G, N])
        q1 = sb("q1", [P, G, N])
        k1r = sb("k1r", [P, G, N], f32r)
        q1r = sb("q1r", [P, G, N], f32r)
        vpad = sb("vpad", [P, NT, H, HP])
        negmax = sb("negmax", [P, 2, G, 2, P])
        q2 = sb("q2", [P, 2, G, S])
        x1 = sb("x1", [P, NT, D])
        qbd = sb("qbd", [P, 2, G, HG, S])
        probs = sb("probs", [P, G, 2, HG, S])
        o_sb = sb("o_sb", [P, G * S])
        rec = sb("rec", [P, 4, HG])
        attn = sb("attn", [P, 2, G, HG * HD])
        attnT = sb("attnT", [P, S])
        bot = sb("bot", [P, D])
        pay = sb("pay", [P, NT, PAY])
        xn2T = sb("xn2T", [P, S])
        xb = sb("xb", [P, NT, D])

        early = sb("early", [P, E * 2 * HID])
        b1_sb = early
        taken = [0]

        def carve(*shape):
            n = 1
            for d in shape:
                n *= d
            v = early[:, taken[0]:taken[0] + n]
            taken[0] += n
            return v.rearrange("p (a b) -> p a b", a=shape[0]) if len(shape) == 2 else v

        ctx_sb, maskkq, xn, x_sb = carve(2, N), carve(2, N), carve(NT, D), carve(NT, D)
        bmv, a_sb = carve(NT, D), carve(A_END)
        wk_sb = a_sb[:, A_WK:A_WK + 2 * G * P].rearrange("p (f o) -> p f o", f=2)
        bqk_sb = a_sb[:, A_BQK:A_BQK + 2 * G].rearrange("p (s g) -> p s g", s=2)
        assert taken[0] <= E * 2 * HID
        mask3b = probs[0:3, 0, 0, :, :].rearrange("p a b -> p (a b)")
        mask3t = q2[0:3, :, :, :].rearrange("p a b c -> p (a b c)")
        gsb, asb = k1[:, 0, :].rearrange("p (a b) -> p a b", a=2), k1[:, 1, :].rearrange("p (a b) -> p a b", a=2)
        sg, u = q1[:, 0, :].rearrange("p (a b) -> p a b", a=2), q1[:, 1, :].rearrange("p (a b) -> p a b", a=2)
        gT = xb[:, :, :].rearrange("p t d -> p (t d)").rearrange("p (a b) -> p a b", a=2)
        lg = sb("lg", [P, 2, E])
        lmax = sb("lmax", [P, 2])
        hit = sb("hit", [P, 2, E])
        key = sb("key", [P, 2, E])
        kmax = sb("kmax", [P, 2])
        onehot = sb("onehot", [P, NT, E], bf16)
        before = sb("before", [P, NT + 1, E], bf16)
        over = sb("over", [P, E, E])
        ntile = sb("ntile", [P, E])
        ends = sb("ends", [P, E])
        place = sb("place", [P, 2, E])
        placed = sb("placed", [P, 2, E])
        posf = sb("posf", [P, 2])
        pos = sb("pos", [P, NT], i32)
        past = sb("past", [P, ROUTED, E])
        npast = sb("npast", [P, ROUTED])
        expert = sb("expert", [P, ROUTED], i32)
        skip = sb("skip", [P, E])
        skipped = sb("skipped", [P, ROUTED, E])
        rowsum = sb("rowsum", [P, ROUTED])
        rowplus = sb("rowplus", [P, ROUTED])
        first_row = sb("first_row", [P, ROUTED], i32)
        fill = sb("fill", [P, PAY])
        xs = sb("xs", [P, 2, PAY])
        ids = sb("ids", [P, ROUTED], i32)
        x1g = sb("x1g", [P, 2, D])
        xT = sb("xT", [P, 2, P])
        yb = sb("yb", [P, 2, D])
        res = sb("res", [P, 2, D])

        bank = [ctx.enter_context(nc.psum_tensor(f"bank{i}", [P, 512], f32)) for i in range(8)]

        x_in, ctx_in, mask_in, a_in, b_in, c_in = map(sem, "x_in ctx_in mask_in a_in b_in c_in".split())
        w1_in, w2_in, b1_in = map(sem, "w1_in w2_in b1_in".split())
        pool_set, chain, pchain, achain = map(sem, "pool_set dve_step pool_step act_step".split())
        mask3_rdy, mask_ps, mask_rdy, var_rdy, rstd_rdy, xn_rdy = map(
            sem, "mask3_rdy mask_ps mask_rdy var_rdy rstd_rdy xn_rdy".split())
        xnT_ps, xnT_rdy, kq_ps, kq_rdy, kqr_rdy, v_ps, v_rdy, bmv_rdy, tg_rdy, xb_rdy = map(
            sem, "xnT_ps xnT_rdy kq_ps kq_rdy kqr_rdy v_ps v_rdy bmv_rdy tg_rdy xb_rdy".split())
        s1_ps, max_rdy, mt_ps, q2_rdy, qbd_rdy, s2_ps, exp_rdy, av_ps, o_rdy = map(
            sem, "s1_ps max_rdy mt_ps q2_rdy qbd_rdy s2_ps exp_rdy av_ps o_rdy".split())
        sum_ps, attn_rdy, proj_ps, var2_rdy, rstd2_rdy, xn2_rdy, xn2T_ps, xn2T_rdy, lg_ps, lg_rdy, hot_rdy = map(
            sem, "sum_ps attn_rdy proj_ps var2_rdy rstd2_rdy xn2_rdy xn2T_ps xn2T_rdy lg_ps lg_rdy hot_rdy".split())
        rank_ps, pos_rdy, expert_rdy, row_rdy, filled, id_rdy, sent, b2t_rdy, x1_rdy, x1_out, maskcol_rdy, col_rdy = map(
            sem, "rank_ps pos_rdy expert_rdy row_rdy filled id_rdy sent b2t_rdy x1_rdy x1_out maskcol_rdy col_rdy".split())
        oT_ps, norm_rdy, aT_ps = map(sem, "oT_ps norm_rdy aT_ps".split())
        ids_rdy, yb_rdy, x1g_clear = map(sem, "ids_rdy yb_rdy x1g_clear".split())
        x1g_in = [sem("x1g_in0"), sem("x1g_in1")]
        xs_in = [sem("xs_in0"), sem("xs_in1")]
        out_done = [sem("out_done0"), sem("out_done1")]
        xT_ps, xT_rdy, hg_ps, ha_ps, g_rdy, a_rdy, sg_rdy, u_rdy, gT_ps, gT_rdy, y_ps, fin_rdy = map(
            sem, "xT_ps xT_rdy hg_ps ha_ps g_rdy a_rdy sg_rdy u_rdy gT_ps gT_rdy y_ps fin_rdy".split())

        block = ctx.enter_context(nc.Block())
        STEPS = range(-2, ROUTED + 1)

        def is_tile(i):
            return 0 <= i < ROUTED

        @block.sync
        def _(sp):
            sp.dma_start(x_sb, x.rearrange("(t p) d -> p t d", p=P)).then_inc(x_in, 16)
            for half in range(2):
                cols = slice(half * 512, half * 512 + 512)
                sp.dma_start(ctx_sb[:, :, cols], ctxT.rearrange("(f p) t -> p f t", p=P)[:, :, cols]).then_inc(ctx_in, 16)
            sp.dma_start(c_sb[:, :], pack_c).then_inc(c_in, 16)
            sp.dma_start(w1_sb[:, :].rearrange("p (e f) -> p e f", e=E), w1.rearrange("e p f -> p e f")).then_inc(w1_in, 16)
            sp.dma_start(w2_sb[:, :].rearrange("p (e c d) -> p e c d", e=E, c=HC),
                         w2.rearrange("e (c p) d -> p e c d", p=P)).then_inc(w2_in, 16)
            sp.wait_ge(v_rdy, NT)
            sp.wait_ge(kq_rdy, 8)
            sp.wait_ge(xb_rdy, 1)
            sp.dma_start(b1_sb[:, :], b1.rearrange("e f -> (e f)").partition_broadcast(P)).then_inc(b1_in, 16)
            sp.dma_start(b2_sb[:, :], b2.rearrange("e f -> (e f)").partition_broadcast(P)).then_inc(b1_in, 16)

            for b in range(B):
                sp.wait_ge(x1_rdy, b + 1)
                sp.dma_start(x1_dram[b * S:(b + 1) * S, :].rearrange("(t p) d -> p t d", p=P),
                             x1[:, 2 * b:2 * b + 2, :]).then_inc(x1_out, 16)

            sp.wait_ge(row_rdy, 1)
            sp.wait_ge(sent, 16 * NT)

            def load(i):
                r = sp.value_load(first_row[0:1, ds(i, 1)], min_val=0, max_val=E * N)
                if i >= 2:
                    sp.wait_ge(xT_ps, i - 1)
                    sp.wait_ge(ids_rdy, i - 1)
                sp.dma_start(xs[:, i % 2, :], slots[ds(r, P), :]).then_inc(xs_in[i % 2], 16)

            for i in range(ROUTED):
                load(i)
            for par in range(2):
                sp.wait_ge(out_done[par], 16 * ((ROUTED + 1 - par) // 2))

        @block.gpsimd
        def _(pool):
            nc.gpsimd.memset(ones_bf[:, :], 1.0).then_inc(pool_set, 1)
            nc.gpsimd.memset(half_neg[:, :], -0.5).then_inc(pool_set, 1)
            nc.gpsimd.memset(fill[:, 0:D], 0.0).then_inc(pool_set, 1)
            nc.gpsimd.iota(fill[:, D:PAY].bitcast(i32), pattern=[[0, 1]], base=NOWHERE,
                           channel_multiplier=0).then_inc(pool_set, 1)
            nc.gpsimd.iota(pay[:, :, D:PAY].bitcast(i32), pattern=[[P, NT], [0, 1]], base=0,
                           channel_multiplier=1).then_inc(id_rdy, 1)

            def inverse_roots(n0, n1, var, tmp, root, ready, value, done):
                pool.wait_ge(ready, value)
                nc.gpsimd.tensor_scalar(tmp[:, n0:n1], var[:, n0:n1, 1], EPS, None, ALU.add).then_inc(pchain, 1)
                pchained[0] += 1
                pool.wait_ge(pchain, pchained[0])
                nc.gpsimd.tensor_tensor(root[:, n0:n1], tmp[:, n0:n1], half_neg[:, n0:n1], ALU.pow).then_inc(done, 1)
            pchained = [0]
            pool.wait_ge(pool_set, 4)
            inverse_roots(0, NT, mv, veps, rstd, var_rdy, 1, rstd_rdy)
            nc.gpsimd.memset(negmax[:, :, :, :, :], 0.0).then_inc(pool_set, 1)
            nc.gpsimd.memset(vpad[:, :, :, HD:HD + 1], 1.0).then_inc(pool_set, 1)
            nc.gpsimd.memset(vpad[:, :, :, HD + 1:HP], 0.0).then_inc(pool_set, 1)
            nc.gpsimd.memset(qbd[:, :, :, :, :], 0.0).then_inc(pool_set, 1)
            nc.gpsimd.memset(x1g[:, :, :], 0.0).then_inc(x1g_clear, 1)
            nc.gpsimd.memset(before[:, 0, :], 0.0).then_inc(pool_set, 1)
            nc.gpsimd.memset(ones_f[:, :], 1.0).then_inc(pool_set, 1)
            pool.wait_ge(a_in, 16)
            nc.gpsimd.tensor_copy(maskcol_sb[:, :], a_sb[:, A_MASK:A_MASK + NT]).then_inc(maskcol_rdy, 1)
            pool.wait_ge(c_in, 16)
            pool.wait_ge(maskcol_rdy, 1)
            nc.gpsimd.tensor_tensor(bmv, bv_sb.unsqueeze(1).broadcast_to([P, NT, D]),
                                    maskcol_sb[:, :].unsqueeze(2).broadcast_to([P, NT, D]), ALU.mult).then_inc(bmv_rdy, 1)
            pool.wait_ge(tg_rdy, 1)
            nc.gpsimd.tensor_scalar(bot[:, :], bo_sb, tg[:, 0:1], None, ALU.mult).then_inc(pchain, 1)
            pchained[0] += 1
            pool.wait_ge(pchain, pchained[0])
            pool.wait_ge(x_in, 16)
            nc.gpsimd.tensor_tensor(xb[:, :, :], x_sb, bot[:, :].unsqueeze(1).broadcast_to([P, NT, D]), ALU.add).then_inc(xb_rdy, 1)
            pool.dma_start(slots.rearrange("(i p) d -> p i d", p=P),
                           fill[:, :].unsqueeze(1).broadcast_to([P, E * N // P + 1, PAY])).then_inc(filled, 16)
            pool.wait_ge(b_in, 16)
            nc.gpsimd.tensor_copy(tri_bf[:, :], b_sb[:, B_TRI:B_TRI + P]).then_inc(pool_set, 1)

            def scatter_rows(b):
                pool.wait_ge(pos_rdy, b + 1)
                for t in range(2 * b, 2 * b + 2):
                    pool.indirect_dma_start(out=slots, out_offset=bass.IndirectOffsetOnAxis(ap=pos[:, t:t + 1], axis=0),
                                            in_=pay[:, t, :], in_offset=None).then_inc(sent, 16)

            for b in range(B):
                if b >= 2:
                    scatter_rows(b - 2)
                inverse_roots(2 * b, 2 * b + 2, mv2, veps2, rstd2, var2_rdy, b + 1, rstd2_rdy)
                if b == 0:
                    pool.wait_ge(b1_in, 32)
                    nc.gpsimd.tensor_scalar(b2_sb[:, :], b2_sb[:, :], tg[:, 1:2], None, ALU.mult).then_inc(b2t_rdy, 1)
                    pool.wait_ge(filled, 16)
                    pool.wait_ge(id_rdy, 1)
            for b in range(B - 2, B):
                scatter_rows(b)
            pool.wait_ge(x1_out, 16 * B)
            pool.wait_ge(x1g_clear, 1)

            for s in STEPS:
                i = s - 1
                if is_tile(i):
                    pool.wait_ge(fin_rdy, i + 1)
                    pool.indirect_dma_start(out=out, out_offset=bass.IndirectOffsetOnAxis(ap=ids[:, i:i + 1], axis=0),
                                            in_=res[:, i % 2, :], in_offset=None, bounds_check=N - 1,
                                            oob_is_err=False).then_inc(out_done[i % 2], 16)
                i = s + 1
                if is_tile(i):
                    pool.wait_ge(ids_rdy, i + 1)
                    pool.indirect_dma_start(out=x1g[:, i % 2, :], out_offset=None, in_=x1_dram,
                                            in_offset=bass.IndirectOffsetOnAxis(ap=ids[:, i:i + 1], axis=0),
                                            bounds_check=N - 1, oob_is_err=False).then_inc(x1g_in[i % 2], 16)

        @block.scalar
        def _(act):
            act.dma_start(m_sb[:, :], mask3).then_inc(mask_in, 16)
            act.dma_start(a_sb, pack_a).then_inc(a_in, 16)
            act.dma_start(b_sb[:, :], pack_b).then_inc(b_in, 16)
            act.wait_ge(pool_set, 1)
            nc.scalar.activation(warm[:, 0:1], ones_bf[0:1, 0:1], ACT.Exp).then_inc(achain, 1)

            for side in range(2):
                act.wait_ge(mask_ps, side + 1)
                for half in range(2):
                    nc.scalar.activation(maskkq[:, side, half * 512:half * 512 + 512], bank[4 + 2 * side + half][:, :],
                                         ACT.Copy).then_inc(mask_rdy, 1)
            for half in range(2):
                act.wait_ge(xnT_ps, half + 1)
                nc.scalar.activation(xnT[:, half * 512:half * 512 + 512], bank[half][:, :], ACT.Copy).then_inc(xnT_rdy, 1)
            act.wait_ge(a_in, 16)
            nc.scalar.activation(tg[:, :], a_sb[:, A_GATES:A_GATES + 2], ACT.Tanh).then_inc(tg_rdy, 1)
            for n, (side, g, half) in enumerate(BLOCKS):
                src, dst = ((k1, k1r), (q1, q1r))[side]
                act.wait_ge(kq_rdy, n + 1)
                nc.scalar.activation(dst[:, g, half * 512:half * 512 + 512], src[:, g, half * 512:half * 512 + 512],
                                     ACT.Copy).then_inc(kqr_rdy, 1)
            act.wait_ge(pool_set, 10)

            def spread_queries(b, heads):
                act.wait_ge(q2_rdy, b + 1)
                if b >= 2:
                    act.wait_ge(s2_ps, 8 * (b - 1))
                for j in heads:
                    nc.scalar.activation(qbd[HP * j:HP * (j + 1), b % 2, :, j, :], q2[HP * j:HP * (j + 1), b % 2, :, :],
                                         ACT.Copy).then_inc(qbd_rdy, 1)

            def exponentials(b, g, ns):
                if b >= 1:
                    act.wait_ge(av_ps, 2 * (b - 1) + g + 1)
                for n in ns:
                    st, hf = n // 2, n % 2
                    m = 8 * b + 4 * g + n
                    act.wait_ge(s2_ps, m + 1)
                    nc.scalar.activation(probs[:, g, st, 2 * hf:2 * hf + 2, :].rearrange("p j t -> p (j t)"),
                                         bank[4 + m % 2][:, :], ACT.Exp, scale=HD ** -0.5).then_inc(exp_rdy, 1)

            spread_queries(0, range(HG))
            for b in range(B + 2):
                if b < B:
                    exponentials(b, 0, [0, 1])
                if b >= 2:
                    act.wait_ge(xn2T_ps, b - 1)
                    nc.scalar.activation(xn2T[:, :], bank[1][:, 0:S], ACT.Copy).then_inc(xn2T_rdy, 1)
                if b < B:
                    exponentials(b, 0, [2, 3])
                if 1 <= b and b + 1 < B:
                    spread_queries(b + 1, [0, 1])
                if b < B:
                    exponentials(b, 1, [0, 1])
                if b == 0:
                    spread_queries(1, [0, 1])
                if 1 <= b <= B:
                    act.wait_ge(aT_ps, b)
                    if b >= 2:
                        act.wait_ge(proj_ps, b - 1)
                    nc.scalar.activation(attnT[:, :], bank[7][:, 0:S], ACT.Copy).then_inc(attn_rdy, 1)
                if b < B:
                    exponentials(b, 1, [2, 3])
                if b + 1 < B:
                    spread_queries(b + 1, [2, 3])
                if b < B:
                    act.wait_ge(av_ps, 2 * b + 2)
                    if b >= 1:
                        act.wait_ge(oT_ps, b)
                    nc.scalar.activation(o_sb[:, :], bank[6][:, :], ACT.Copy).then_inc(o_rdy, 1)
                if b == B - 1:
                    nc.scalar.activation(warm[:, 1:2], ones_bf[0:1, 0:1], ACT.Sigmoid).then_inc(achain, 1)

            for s in STEPS:
                i = s + 2
                if is_tile(i):
                    act.wait_ge(xT_ps, i + 1)
                    if i >= 2:
                        act.wait_ge(ha_ps, i - 1)
                    nc.scalar.activation(xT[:, i % 2, :], bank[4][:, 0:P], ACT.Copy).then_inc(xT_rdy, 1)
                i = s + 1
                if is_tile(i):
                    act.wait_ge(g_rdy, i + 1)
                    if i >= 2:
                        act.wait_ge(u_rdy, i - 1)
                    nc.scalar.activation(sg[:, i % 2, :], gsb[:, i % 2, :], ACT.Sigmoid).then_inc(sg_rdy, 1)
                i = s
                if is_tile(i):
                    act.wait_ge(gT_ps, i + 1)
                    if i >= 2:
                        act.wait_ge(y_ps, i - 1)
                    nc.scalar.activation(gT[:, i % 2, :], bank[5][:, :], ACT.Copy).then_inc(gT_rdy, 1)

        @block.vector
        def _(dve):
            linked = [0]

            def link(ins):
                ins.then_inc(chain, 1)
                linked[0] += 1
                dve.wait_ge(chain, linked[0])

            dve.wait_ge(mask_in, 16)
            link(nc.vector.tensor_scalar(mask3t[:, :], mask3_sb[:, :], 0.0, clear3_sb[:, 0:1], ALU.is_equal, ALU.mult))
            nc.vector.scalar_tensor_tensor(mask3b[:, :], mask3_sb[:, :], clear3_sb[:, 1:2], mask3t[:, :],
                                           ALU.mult, ALU.add).then_inc(mask3_rdy, 1)

            dve.wait_ge(x_in, 16)
            for t in range(NT):
                last = nc.vector.bn_stats(stats[:, t, :], x_sb[:, t, :])
                if t < NT - 1:
                    last.then_inc(chain, 1)
                    linked[0] += 1
            link(last)
            for t in range(NT):
                last = nc.vector.bn_aggr(mv[:, t, :], stats[:, t, :])
            last.then_inc(var_rdy, 1)
            dve.wait_ge(var_rdy, 1)
            dve.wait_ge(rstd_rdy, 1)
            for t in range(NT):
                nc.vector.tensor_scalar(xn[:, t, :], x_sb[:, t, :], mv[:, t, 0:1], rstd[:, t:t + 1],
                                        ALU.subtract, ALU.mult).then_inc(xn_rdy, 1)
            def keys_queries(n):
                side, g, half = BLOCKS[n]
                cols = slice(half * 512, half * 512 + 512)
                dve.wait_ge(kq_ps, n + 1)
                nc.vector.scalar_tensor_tensor((k1, q1)[side][:, g, cols], bank[KQ_BANK[n]][:, :],
                                               bqk_sb[:, 1 - side, g:g + 1], maskkq[:, side, cols],
                                               ALU.add, ALU.mult).then_inc(kq_rdy, 1)

            def values():
                dve.wait_ge(bmv_rdy, 1)
                for t in range(NT):
                    dve.wait_ge(v_ps, t // 4 + 1)
                    nc.vector.scalar_tensor_tensor(vpad[:, t, :, 0:HD],
                                                   bank[V_BANK[t // 4]][:, t % 4 * D:t % 4 * D + D].rearrange("p (h d) -> p h d", h=H),
                                                   maskcol_sb[:, t:t + 1], bmv[:, t, :].rearrange("p (h d) -> p h d", h=H),
                                                   ALU.mult, ALU.add).then_inc(v_rdy, 1)

            def maxima(b, g, heads=range(HG)):
                if b >= 2 and g == 0:
                    dve.wait_ge(mt_ps, b - 1)
                for j in heads:
                    dve.wait_ge(s1_ps, (2 * b + g) * HG + j + 1)
                    nc.vector.tensor_reduce(negmax[:, b % 2, g, :, HP * j + HD], bank[j][:, :].rearrange("p (t s) -> p t s", t=2),
                                            AX.X, ALU.max, negate=True).then_inc(max_rdy, 1)

            def shift_queries(b):
                dve.wait_ge(mt_ps, b + 1)
                if b >= 2:
                    dve.wait_ge(qbd_rdy, HG * (b - 1))
                nc.vector.tensor_tensor(q2[:, b % 2, :, :], q1[:, :, b * S:(b + 1) * S],
                                        bank[3][:, :].rearrange("p (g t) -> p g t", g=G), ALU.add).then_inc(q2_rdy, 1)

            def normalise(b):
                dve.wait_ge(oT_ps, b + 1)
                o = bank[7][:, :].rearrange("p (n j c) -> p n j c", n=4, j=HG)
                link(nc.vector.reciprocal(rec[:, :, :], o[:, :, :, HD]))
                if b >= 1:
                    dve.wait_ge(aT_ps, b)
                for g in range(G):
                    nc.vector.tensor_tensor(attn[:, :, g, :].rearrange("p t (j d) -> p t j d", j=HG),
                                            o[:, 2 * g:2 * g + 2, :, 0:HD],
                                            rec[:, 2 * g:2 * g + 2, :].unsqueeze(3).broadcast_to([P, 2, HG, HD]),
                                            ALU.mult).then_inc(norm_rdy, 1)

            def residual(b):
                dve.wait_ge(proj_ps, b + 1)
                dve.wait_ge(xb_rdy, 1)
                nc.vector.scalar_tensor_tensor(x1[:, 2 * b:2 * b + 2, :],
                                               bank[7][:, 0:2 * D].rearrange("p (t d) -> p t d", t=2), tg[:, 0:1],
                                               xb[:, 2 * b:2 * b + 2, :], ALU.mult, ALU.add).then_inc(x1_rdy, 1)
                dve.wait_ge(x1_rdy, b + 1)
                nc.vector.bn_stats(stats2[:, 2 * b, :], x1[:, 2 * b, :]).then_inc(chain, 1)
                linked[0] += 1
                link(nc.vector.bn_stats(stats2[:, 2 * b + 1, :], x1[:, 2 * b + 1, :]))
                nc.vector.bn_aggr(mv2[:, 2 * b, :], stats2[:, 2 * b, :])
                nc.vector.bn_aggr(mv2[:, 2 * b + 1, :], stats2[:, 2 * b + 1, :]).then_inc(var2_rdy, 1)

            def second_norm(b):
                dve.wait_ge(var2_rdy, b + 1)
                dve.wait_ge(rstd2_rdy, b + 1)
                for t in range(2 * b, 2 * b + 2):
                    nc.vector.tensor_scalar(pay[:, t, 0:D], x1[:, t, :], mv2[:, t, 0:1], rstd2[:, t:t + 1],
                                            ALU.subtract, ALU.mult).then_inc(xn2_rdy, 1)

            def route(b):
                dve.wait_ge(lg_ps, b + 1)
                nc.vector.tensor_tensor(lg[:, :, :], bank[2][:, 0:2 * E].rearrange("p (t e) -> p t e", t=2),
                                        rb_sb[:, :].unsqueeze(1).broadcast_to([P, 2, E]), ALU.add).then_inc(lg_rdy, 1)
                dve.wait_ge(lg_rdy, b + 1)
                link(nc.vector.tensor_reduce(lmax[:, :], lg[:, :, :], AX.X, ALU.max))
                link(nc.vector.tensor_tensor(hit[:, :, :], lg[:, :, :], lmax[:, :].unsqueeze(2).broadcast_to([P, 2, E]), ALU.is_equal))
                link(nc.vector.tensor_tensor(key[:, :, :], hit[:, :, :],
                                             b_sb[:, B_PRI:B_PRI + E].unsqueeze(1).broadcast_to([P, 2, E]), ALU.mult))
                link(nc.vector.tensor_reduce(kmax[:, :], key[:, :, :], AX.X, ALU.max))
                nc.vector.tensor_tensor(onehot[:, 2 * b:2 * b + 2, :], key[:, :, :],
                                        kmax[:, :].unsqueeze(2).broadcast_to([P, 2, E]), ALU.is_equal).then_inc(hot_rdy, 1)

            def places(b):
                dve.wait_ge(hot_rdy, b + 1)
                for t in range(2 * b, 2 * b + 2):
                    nc.vector.tensor_tensor(before[:, t + 1, :], before[:, t, :], onehot[:, t, :], ALU.add).then_inc(col_rdy, 1)
                    dve.wait_ge(col_rdy, t + 1)
                dve.wait_ge(rank_ps, b + 1)
                link(nc.vector.tensor_tensor(place[:, :, :], bank[2][:, 32:32 + 2 * E].rearrange("p (t e) -> p t e", t=2),
                                             b_sb[:, B_ROW:B_ROW + 2 * E].rearrange("p (t e) -> p t e", t=2), ALU.add))
                link(nc.vector.tensor_tensor(placed[:, :, :], place[:, :, :], onehot[:, 2 * b:2 * b + 2, :], ALU.mult))
                link(nc.vector.tensor_reduce(posf[:, :], placed[:, :, :], AX.X, ALU.add))
                nc.vector.tensor_copy(pos[:, 2 * b:2 * b + 2], posf[:, :]).then_inc(pos_rdy, 1)

            dve.wait_ge(a_in, 16)
            dve.wait_ge(mask_rdy, 4)
            for n in range(6):
                keys_queries(n)
            dve.wait_ge(pool_set, 10)
            maxima(0, 0)
            keys_queries(6)
            keys_queries(7)
            maxima(0, 1)
            shift_queries(0)
            values()
            maxima(1, 0)
            maxima(1, 1)
            dve.wait_ge(b_in, 16)
            for b in range(B + 2):
                if b >= 2:
                    route(b - 2)
                if b + 1 < B:
                    shift_queries(b + 1)
                if 1 <= b <= B:
                    normalise(b - 1)
                if b >= 2:
                    places(b - 2)
                if b + 2 < B:
                    maxima(b + 2, 0)
                if 1 <= b <= B:
                    residual(b - 1)
                if b + 2 < B:
                    maxima(b + 2, 1, [0, 1])
                if 1 <= b <= B:
                    second_norm(b - 1)
                if b + 2 < B:
                    maxima(b + 2, 1, [2, 3])

            total = bank[0][:, 0:E]
            link(nc.vector.tensor_tensor(over[:, :, :], total.unsqueeze(2).broadcast_to([P, E, E]),
                                         b_sb[:, B_THR:B_THR + E * E].rearrange("p (e k) -> p e k", e=E), ALU.is_gt))
            link(nc.vector.tensor_reduce(ntile[:, :], over[:, :, :], AX.X, ALU.add))
            nc.vector.tensor_scalar(skip[:, :], ntile[:, :], -float(P), float(N), ALU.mult, ALU.add).then_inc(chain, 1)
            linked[0] += 1
            link(nc.vector.tensor_tensor_scan(ends[:, :], ones_f[:, :], ntile[:, :], 0.0, ALU.mult, ALU.add))
            link(nc.vector.tensor_tensor(past[:, :, :], ends[:, :].unsqueeze(1).broadcast_to([P, ROUTED, E]),
                                         b_sb[:, B_TILE:B_TROW].rearrange("p (i e) -> p i e", i=ROUTED), ALU.is_le))
            link(nc.vector.tensor_tensor(skipped[:, :, :], past[:, :, :], skip[:, :].unsqueeze(1).broadcast_to([P, ROUTED, E]),
                                         ALU.mult))
            link(nc.vector.tensor_reduce(rowsum[:, :], skipped[:, :, :], AX.X, ALU.add))
            link(nc.vector.tensor_tensor(rowplus[:, :], rowsum[:, :], b_sb[:, B_TROW:B_END], ALU.add))
            nc.vector.tensor_scalar(first_row[:, :], rowplus[:, :], float(E * N), None, ALU.min).then_inc(row_rdy, 1)
            link(nc.vector.tensor_reduce(npast[:, :], past[:, :, :], AX.X, ALU.add))
            nc.vector.tensor_scalar(expert[:, :], npast[:, :], float(E - 1), None, ALU.min).then_inc(expert_rdy, 1)
            dve.wait_ge(expert_rdy, 1)
            dve.wait_ge(b2t_rdy, 1)

            def dve_expert(i):
                return dve.value_load(expert[0:1, i:i + 1], min_val=0, max_val=E - 1)

            e = []
            for s in STEPS:
                i = s + 2
                if is_tile(i):
                    dve.wait_ge(xs_in[i % 2], 16 * (i // 2 + 1))
                    nc.vector.tensor_copy(ids[:, ds(i, 1)], xs[:, i % 2, D:PAY].bitcast(i32)).then_inc(ids_rdy, 1)
                i = s + 1
                if is_tile(i):
                    if i == 0:
                        dve.wait_ge(b1_in, 32)
                    if i == 0:
                        e.append(dve_expert(0))
                    dve.wait_ge(hg_ps, i + 1)
                    nc.vector.tensor_tensor(gsb[:, i % 2, :], bank[2 * (i % 2)][:, :],
                                            b1_sb[:, ds(e[i] * (2 * HID) + HID, HID)], ALU.add).then_inc(g_rdy, 1)
                    dve.wait_ge(ha_ps, i + 1)
                    nc.vector.tensor_tensor(asb[:, i % 2, :], bank[2 * (i % 2) + 1][:, :],
                                            b1_sb[:, ds(e[i] * (2 * HID), HID)], ALU.add).then_inc(a_rdy, 1)
                    if i + 1 < ROUTED:
                        e.append(dve_expert(i + 1))
                    dve.wait_ge(a_rdy, i + 1)
                    dve.wait_ge(sg_rdy, i + 1)
                    if i >= 2:
                        dve.wait_ge(gT_ps, i - 1)
                    nc.vector.tensor_tensor(u[:, i % 2, :], asb[:, i % 2, :], sg[:, i % 2, :], ALU.mult).then_inc(u_rdy, 1)
                i = s - 1
                if is_tile(i):
                    dve.wait_ge(y_ps, i + 1)
                    nc.vector.scalar_tensor_tensor(yb[:, i % 2, :], bank[6 + i % 2][:, 0:D], tg[:, 1:2],
                                                   b2_sb[:, ds(e[i] * D, D)], ALU.mult, ALU.add).then_inc(yb_rdy, 1)
                    dve.wait_ge(x1g_in[i % 2], 16 * (i // 2 + 1))
                    if i >= 2:
                        dve.wait_ge(out_done[i % 2], 16 * (i // 2))
                    dve.wait_ge(yb_rdy, i + 1)
                    nc.vector.tensor_tensor(res[:, i % 2, :], yb[:, i % 2, :], x1g[:, i % 2, :],
                                            ALU.add).then_inc(fin_rdy, 1)

        @block.tensor
        def _(pe):
            pe.wait_ge(pool_set, 1)
            for n in range(24):
                nc.tensor.matmul(bank[0][:, 0:P], ones_bf[:, :], ones_bf[:, :], start=True, stop=True)
            pe.wait_ge(mask3_rdy, 1)
            for side in range(2):
                for half in range(2):
                    mm = nc.tensor.matmul(bank[4 + 2 * side + half][:, :], sel3_sb[:, side, :],
                                          mask3b[:, half * 512:half * 512 + 512], start=True, stop=True)
                mm.then_inc(mask_ps, 1)

            def project(n):
                side, g, half = BLOCKS[n]
                cols = slice(half * 512, half * 512 + 512)
                if side == 0:
                    for f in range(2):
                        mm = nc.tensor.matmul(bank[KQ_BANK[n]][:, :], wk_sb[:, f, g * P:(g + 1) * P], ctx_sb[:, f, cols],
                                              start=f == 0, stop=f == 1)
                else:
                    mm = nc.tensor.matmul(bank[KQ_BANK[n]][:, :], wq_sb[:, g * P:(g + 1) * P], xnT[:, cols], start=True, stop=True)
                mm.then_inc(kq_ps, 1)

            pe.wait_ge(a_in, 16)
            pe.wait_ge(ctx_in, 32)
            project(0)
            project(1)
            pe.wait_ge(mask_rdy, 4)
            project(2)
            project(3)
            pe.wait_ge(b_in, 16)
            for t in range(NT):
                pe.wait_ge(xn_rdy, t + 1)
                mm = nc.tensor.transpose(bank[t // 4][:, t % 4 * P:t % 4 * P + P], xn[:, t, :], ident)
                if t % 4 == 3:
                    mm.then_inc(xnT_ps, 1)
            pe.wait_ge(xnT_rdy, 1)
            project(4)
            project(5)
            pe.wait_ge(xnT_rdy, 2)
            pe.wait_ge(kq_rdy, 4)
            project(6)
            project(7)

            def project_values():
                pe.wait_ge(c_in, 16)
                pe.wait_ge(kq_rdy, 6)
                for t in range(NT):
                    for f in range(2):
                        mm = nc.tensor.matmul(bank[V_BANK[t // 4]][:, t % 4 * D:t % 4 * D + D], ctx_sb[:, f, t * P:(t + 1) * P],
                                              wv_sb[:, f, :], start=f == 0, stop=f == 1)
                    if t % 4 == 3:
                        mm.then_inc(v_ps, 1)

            def scores_for_max(b, groups=range(G)):
                for g in groups:
                    n = 2 * b + g
                    for tt in range(2):
                        for j in range(HG):
                            if tt == 0 and n >= 1:
                                pe.wait_ge(max_rdy, (n - 1) * HG + j + 1)
                            if tt == 0 and g == 0 and j == 2 and b >= 4:
                                pe.wait_ge(pos_rdy, b - 3)
                            if tt == 0 and g == 0 and j == 3 and b >= 1:
                                pe.wait_ge(q2_rdy, b)
                            q0 = b * S + tt * P
                            mm = nc.tensor.matmul(bank[j][:, tt * S:(tt + 1) * S], q1r[HP * j:HP * (j + 1), g, q0:q0 + P],
                                                  k1r[HP * j:HP * (j + 1), g, b * S:(b + 1) * S], start=True, stop=True)
                            if tt == 1:
                                mm.then_inc(s1_ps, 1)

            def transpose_max(b):
                pe.wait_ge(max_rdy, 2 * HG * (b + 1))
                for g in range(G):
                    for tt in range(2):
                        c = (2 * g + tt) * P
                        mm = nc.tensor.transpose(bank[3][:, c:c + P], negmax[:, b % 2, g, tt, :], ident)
                mm.then_inc(mt_ps, 1)

            def scores(b, g, ns):
                pe.wait_ge(qbd_rdy, HG * (b + 1))
                for n in ns:
                    st, hf = n // 2, n % 2
                    m = 8 * b + 4 * g + n
                    if m >= 2:
                        pe.wait_ge(exp_rdy, m - 1)
                    k0 = b * S + st * P
                    nc.tensor.matmul(bank[4 + m % 2][:, :], k1[:, g, k0:k0 + P],
                                     qbd[:, b % 2, g, 2 * hf:2 * hf + 2, :].rearrange("p j t -> p (j t)"),
                                     start=True, stop=True).then_inc(s2_ps, 1)

            def values(b, g):
                if g == 0 and b >= 1:
                    pe.wait_ge(o_rdy, b)
                for st in range(2):
                    pe.wait_ge(exp_rdy, 8 * b + 4 * g + 2 * st + 2)
                    for j in range(HG):
                        mm = nc.tensor.matmul(bank[6][HP * j:HP * (j + 1), g * S:(g + 1) * S], vpad[:, 2 * b + st, HG * g + j, :],
                                              probs[:, g, st, j, :], start=st == 0, stop=st == 1)
                mm.then_inc(av_ps, 1)

            def transpose_output(b):
                pe.wait_ge(o_rdy, b + 1)
                if b >= 1:
                    pe.wait_ge(x1_rdy, b)
                for n in range(4):
                    mm = nc.tensor.transpose(bank[7][:, n * P:(n + 1) * P], o_sb[:, n * P:(n + 1) * P], ident)
                mm.then_inc(oT_ps, 1)

            def transpose_attention(b):
                pe.wait_ge(norm_rdy, 2 * (b + 1))
                for tt in range(2):
                    mm = nc.tensor.transpose(bank[7][:, tt * P:(tt + 1) * P], attn[:, tt, :, :].rearrange("p g c -> p (g c)"), ident)
                mm.then_inc(aT_ps, 1)

            def output_projection(b):
                pe.wait_ge(attn_rdy, b + 1)
                for tt in range(2):
                    t0 = b * S + tt * P
                    o = bank[7][:, tt * D:(tt + 1) * D]
                    nc.tensor.matmul(o, xnT[:, t0:t0 + P], wox_sb, start=True, stop=False)
                    mm = nc.tensor.matmul(o, attnT[:, tt * P:(tt + 1) * P], woa_sb, start=False, stop=True)
                mm.then_inc(proj_ps, 1)

            def transpose_norm(b):
                pe.wait_ge(xn2_rdy, 2 * (b + 1))
                pe.wait_ge(max_rdy, 2 * HG * min(b + 4, B))
                for tt in range(2):
                    mm = nc.tensor.transpose(bank[1][:, tt * P:tt * P + P], pay[:, 2 * b + tt, 0:D], ident)
                mm.then_inc(xn2T_ps, 1)

            def router(b):
                pe.wait_ge(xn2T_rdy, b + 1)
                for tt in range(2):
                    mm = nc.tensor.matmul(bank[2][:, tt * E:(tt + 1) * E], xn2T[:, tt * P:(tt + 1) * P], rw_sb,
                                          start=True, stop=True)
                mm.then_inc(lg_ps, 1)

            def ranks(b):
                pe.wait_ge(hot_rdy, b + 1)
                pe.wait_ge(pool_set, 11)
                r = bank[2][:, 32:32 + 2 * E].rearrange("p (t e) -> p t e", t=2)
                nc.tensor.matmul(r, tri_bf[:, :], onehot[:, 2 * b:2 * b + 2, :], start=True, stop=False)
                pe.wait_ge(col_rdy, 2 * b + 1)
                mm = nc.tensor.matmul(r, ones_bf[:, :], before[:, 2 * b:2 * b + 2, :], start=False, stop=True)
                if b == B - 1:
                    pe.wait_ge(col_rdy, NT)
                    mm = nc.tensor.matmul(bank[0][:, 0:E], ones_bf[:, :], before[:, NT, :], start=True, stop=True)
                mm.then_inc(rank_ps, 1)

            pe.wait_ge(kqr_rdy, 6)
            scores_for_max(0, [0])
            project_values()
            scores_for_max(0, [1])
            transpose_max(0)
            pe.wait_ge(kqr_rdy, 8)
            scores_for_max(1, [0])
            for b in range(B + 2):
                if b < B:
                    scores(b, 0, [0, 1])
                if b >= 2:
                    transpose_norm(b - 2)
                if b < B:
                    scores(b, 0, [2])
                if b >= 2:
                    router(b - 2)
                if b < B:
                    scores(b, 0, [3])
                if b == 0:
                    scores_for_max(1, [1])
                elif b + 1 < B:
                    transpose_max(b + 1)
                if 1 <= b <= B:
                    transpose_output(b - 1)
                if b < B:
                    pe.wait_ge(v_rdy, NT)
                    values(b, 0)
                if b >= 2:
                    ranks(b - 2)
                if b < B:
                    scores(b, 1, [0, 1])
                if b == 0:
                    transpose_max(1)
                if 1 <= b <= B:
                    transpose_attention(b - 1)
                if b + 2 < B:
                    scores_for_max(b + 2, [0])
                if b < B:
                    scores(b, 1, [2, 3])
                if 1 <= b <= B:
                    output_projection(b - 1)
                if b < B:
                    values(b, 1)
                if b + 2 < B:
                    scores_for_max(b + 2, [1])

            def pe_expert(i):
                return pe.value_load(expert[0:1, i:i + 1], min_val=0, max_val=E - 1)

            e = []
            for s in STEPS:
                i = s + 2
                if is_tile(i):
                    pe.wait_ge(xs_in[i % 2], 16 * (i // 2 + 1))
                    if i >= 1:
                        pe.wait_ge(xT_rdy, i)
                    nc.tensor.transpose(bank[4][:, 0:P], xs[:, i % 2, 0:D], ident).then_inc(xT_ps, 1)
                i = s + 1
                if is_tile(i):
                    if i == 0:
                        pe.wait_ge(w1_in, 16)
                        pe.wait_ge(expert_rdy, 1)
                        e.append(pe_expert(0))
                    pe.wait_ge(xT_rdy, i + 1)
                    if i >= 2:
                        pe.wait_ge(a_rdy, i - 1)
                    nc.tensor.matmul(bank[2 * (i % 2)][:, :], xT[:, i % 2, :], w1_sb[:, ds(e[i] * (2 * HID) + HID, HID)],
                                     start=True, stop=True).then_inc(hg_ps, 1)
                    nc.tensor.matmul(bank[2 * (i % 2) + 1][:, :], xT[:, i % 2, :], w1_sb[:, ds(e[i] * (2 * HID), HID)],
                                     start=True, stop=True).then_inc(ha_ps, 1)
                    if i + 1 < ROUTED:
                        e.append(pe_expert(i + 1))
                i = s
                if is_tile(i):
                    pe.wait_ge(u_rdy, i + 1)
                    if i >= 1:
                        pe.wait_ge(gT_rdy, i)
                    for c in range(HC):
                        mm = nc.tensor.transpose(bank[5][:, c * P:(c + 1) * P], u[:, i % 2, c * P:(c + 1) * P], ident)
                    mm.then_inc(gT_ps, 1)
                i = s - 1
                if is_tile(i):
                    if i == 0:
                        pe.wait_ge(w2_in, 16)
                    pe.wait_ge(gT_rdy, i + 1)
                    if i >= 2:
                        pe.wait_ge(fin_rdy, i - 1)
                    for c in range(HC):
                        mm = nc.tensor.matmul(bank[6 + i % 2][:, 0:D], gT[:, i % 2, c * P:(c + 1) * P],
                                              w2_sb[:, ds(e[i] * (HC * D) + c * D, D)], start=c == 0, stop=c == HC - 1)
                    mm.then_inc(y_ps, 1)


BLOCKS = [(0, 0, 0), (0, 1, 0), (0, 0, 1), (0, 1, 1), (1, 0, 0), (1, 1, 0), (1, 0, 1), (1, 1, 1)]
KQ_BANK = [2, 3, 4, 5, 6, 7, 4, 5]
V_BANK = [6, 7]


def pad_heads(a):
    import numpy as np
    a = a.reshape(a.shape[:-1] + (H, HD))
    return np.concatenate([a, np.zeros(a.shape[:-1] + (HP - HD,), a.dtype)], -1).reshape(a.shape[:-2] + (H * HP,))


def shape_constants():
    import numpy as np
    f = np.float32
    c = np.zeros((P, B_END - B_TRI), f)
    o = -B_TRI
    c[:, o + B_TRI:o + B_TRI + P] = np.triu(np.ones((P, P), f), 1)
    c[:, o + B_THR:o + B_THR + E * E] = np.tile(np.arange(E) * P, E)
    c[:, o + B_PRI:o + B_PRI + E] = E - np.arange(E)
    c[:, o + B_ROW:o + B_ROW + 2 * E] = np.tile(np.arange(E) * N, 2)
    c[:, o + B_TILE:o + B_TROW] = np.repeat(np.arange(ROUTED), E)
    c[:, o + B_TROW:o + B_END] = np.arange(ROUTED) * P
    row = np.arange(P) % HP
    sel3 = np.zeros((3, 2, P), f)
    sel3[0, :, row < HD] = 1
    sel3[2, 0, row == HD] = 1
    sel3[1, 0, row == HD + 1] = 1
    sel3[2, 1, row == HD + 1] = 1
    clear3 = np.array([[0, 1], [MASKED, 0], [0, 1]], f)
    return c, np.concatenate([sel3.reshape(3, 2 * P), clear3], 1)


def kernel(x, ctx_2048, mask_BxS2_fk1, g_xattn, g_ffn, L0_xattn_W_src, L0_xattn_b_src, L0_xattn_W_tgt, L0_xattn_b_tgt,
           L0_xattn_W_out, L0_xattn_b_out, L0_ffn_router_w, L0_ffn_router_b, L0_ffn_w1, L0_ffn_b1, L0_ffn_w2, L0_ffn_b2):
    import numpy as np
    import concourse.bacc as bacc
    from concourse.bass_utils import run_bass_kernel_spmd as run

    a = np.asarray
    consts, sel3 = shape_constants()
    mask = a(mask_BxS2_fk1).reshape(1, N)
    w_src, b_src, w_out = a(L0_xattn_W_src), a(L0_xattn_b_src), a(L0_xattn_W_out)
    row = np.arange(P) % HP
    bq = pad_heads(a(L0_xattn_b_tgt)).reshape(G, P).T.copy()
    bk = pad_heads(b_src[:D]).reshape(G, P).T.copy()
    bq[row == HD + 1] = 1
    bk[(row == HD) | (row == HD + 1)] = 1

    def by_rows(m):
        return m.reshape(-1, P, m.shape[1]).transpose(1, 0, 2).reshape(P, -1)

    def on_all(v):
        return np.broadcast_to(v, (P, v.size))

    arrays = {
        "x": a(x).reshape(N, D),
        "ctxT": a(ctx_2048).reshape(N, F).T,
        "mask3": np.concatenate([np.concatenate([mask, mask, np.ones_like(mask)]), sel3], 1),
        "pack_a": np.concatenate([by_rows(pad_heads(w_src[:D].T)), bq, bk, mask.reshape(NT, P).T,
                                  on_all(a(g_xattn)), on_all(a(g_ffn))], 1),
        "pack_b": np.concatenate([np.eye(P, dtype=np.float32), pad_heads(a(L0_xattn_W_tgt).T), a(L0_ffn_router_w),
                                  on_all(a(L0_ffn_router_b)), consts], 1),
        "pack_c": np.concatenate([by_rows(w_src[D:].T), w_out[:, :D].T, w_out[:, D:].T, on_all(b_src[D:]),
                                  on_all(a(L0_xattn_b_out))], 1),
        "w1": a(L0_ffn_w1), "b1": a(L0_ffn_b1), "w2": a(L0_ffn_w2), "b2": a(L0_ffn_b2),
    }
    nc = bacc.Bacc("TRN2", target_bir_lowering=False, num_devices=1)
    arrays = {f"in_{k}": np.ascontiguousarray(v) for k, v in arrays.items()}
    args = [nc.dram_tensor(k, v.shape, mybir.dt.from_np(v.dtype), kind="ExternalInput").ap() for k, v in arrays.items()]
    out = nc.dram_tensor("out_0", (N, D), mybir.dt.float32, kind="ExternalOutput").ap()
    build(nc, *args, out)
    r = run(nc, [arrays], core_ids=[0])
    return np.asarray(r.results[0]["out_0"]).reshape(B, S, D)
```

```python
import concourse.bass as bass
from concourse import mybir
from contextlib import ExitStack

B, S, D, F = 4, 256, 128, 256
H, HD = 8, 16
HP = 32
G, HG = 2, 4
P = 128
N = B * S
NT = N // P
E, HID = 8, 512
ROUTED = NT + E - 1
HC = HID // P
PAY = D + 1
EPS = 1e-5
MASKED = -2.0 ** 100
FILL_ROWS = 5
NOWHERE = 4 * N
A_ID, A_WK, A_BQK, A_MASK, A_GATES, A_END = 0, 128, 640, 644, 652, 654
B_WQ, B_RW, B_RB, B_TRI, B_THR, B_PRI, B_ROW, B_TILE, B_TROW = 0, 256, 264, 272, 400, 464, 472, 488, 608
B_END = 623
C_WV, C_WOX, C_WOA, C_BV, C_BO, C_END = 0, 256, 384, 512, 640, 768
VPAD_SET, QBD_SET, FILL_SET, ALL_SET = 5, 6, 8, 12
WARM_UP, FFN_WARM_UP = 58, 74
assert B_TROW + ROUTED == B_END


def build(nc, x, ctxT, mask_row, key_mask, query_mask, pack_a, pack_b, pack_c, w1, b1, w2, b2, out):
    f32, f32r, bf16, i32 = mybir.dt.float32, mybir.dt.float32r, mybir.dt.bfloat16, mybir.dt.int32
    ALU, ACT, AX = mybir.AluOpType, mybir.ActivationFunctionType, mybir.AxisListType
    ds = bass.ds
    slots = nc.dram_tensor("slots", (E * N + P, PAY), f32).ap()
    x1_dram = nc.dram_tensor("x1_dram", (N, D), f32).ap()

    with ExitStack() as ctx:
        def sb(name, shape, dt=f32):
            return ctx.enter_context(nc.sbuf_tensor(name, shape, dt))

        def sem(name):
            return ctx.enter_context(nc.semaphore(name))

        a_sb = sb("a_sb", [P, A_END])
        ident = a_sb[:, A_ID:A_ID + P]
        b_sb = sb("b_sb", [P, B_END])
        wq_sb = b_sb[:, B_WQ:B_WQ + G * P]
        rw_sb, rb_sb = b_sb[:, B_RW:B_RW + E], b_sb[:, B_RB:B_RB + E]
        c_sb = sb("c_sb", [P, C_END])
        wv_sb = c_sb[:, C_WV:C_WV + 2 * D].rearrange("p (f d) -> p f d", f=2)
        wox_sb, woa_sb = c_sb[:, C_WOX:C_WOX + D], c_sb[:, C_WOA:C_WOA + D]
        bv_sb, bo_sb = c_sb[:, C_BV:C_BV + D], c_sb[:, C_BO:C_BO + D]
        maskcol_sb = sb("maskcol_sb", [P, NT])
        tg = sb("tg", [P, 2])
        warm = sb("warm", [1, 2])
        w1_sb = sb("w1_sb", [P, E * 2 * HID])
        w2_sb = sb("w2_sb", [P, E * HC * D])
        b2_sb = sb("b2_sb", [P, E * D])
        tri_bf = sb("tri_bf", [P, P], bf16)
        ones_bf = sb("ones_bf", [P, P], bf16)
        ones_f = sb("ones_f", [P, E])
        stats = sb("stats", [P, NT, 6])
        mv = sb("mv", [P, NT, 2])
        veps = sb("veps", [P, NT])
        rstd = sb("rstd", [P, NT])
        stats2 = sb("stats2", [P, NT, 6])
        mv2 = sb("mv2", [P, NT, 2])
        veps2 = sb("veps2", [P, NT])
        rstd2 = sb("rstd2", [P, NT])
        half_neg = sb("half_neg", [P, NT])
        xnT = sb("xnT", [P, N])
        k1 = sb("k1", [P, G, N])
        q1 = sb("q1", [P, G, N])
        k1r = sb("k1r", [P, G, N], f32r)
        q1r = sb("q1r", [P, G, N], f32r)
        vpad = sb("vpad", [P, NT, H, HP])
        negmax = sb("negmax", [P, 2, G, 2, P])
        q2 = sb("q2", [P, 2, G, S])
        x1 = sb("x1", [P, NT, D])
        qbd = sb("qbd", [P, 2, G, HG, S])
        probs = sb("probs", [P, G, 2, HG, S])
        o_sb = sb("o_sb", [P, G * S])
        rec = sb("rec", [P, 4, HG])
        attn = sb("attn", [P, 2, G, HG * HD])
        attnT = sb("attnT", [P, S])
        bot = sb("bot", [P, D])
        pay = sb("pay", [P, NT, PAY])
        xn2T = sb("xn2T", [P, S])
        xb = sb("xb", [P, NT, D])

        early = sb("early", [P, E * 2 * HID])
        b1_sb = early
        taken = [0]

        def carve(*shape):
            n = 1
            for d in shape:
                n *= d
            v = early[:, taken[0]:taken[0] + n]
            taken[0] += n
            return v.rearrange("p (a b) -> p a b", a=shape[0]) if len(shape) == 2 else v

        ctx_sb, maskkq, xn, x_sb = carve(2, N), carve(2, N), carve(NT, D), carve(NT, D)
        bmv = carve(NT, D)
        wk_sb = a_sb[:, A_WK:A_WK + 2 * G * P].rearrange("p (f o) -> p f o", f=2)
        bqk_sb = a_sb[:, A_BQK:A_BQK + 2 * G].rearrange("p (s g) -> p s g", s=2)
        assert taken[0] <= E * 2 * HID
        mask4, masked4 = [probs[0:HG, g, 0, :, :].rearrange("p j t -> p (j t)") for g in range(2)]
        fill = b2_sb[:, 0:FILL_ROWS * PAY].rearrange("p (k d) -> p k d", k=FILL_ROWS)
        gsb, asb = k1[:, 0, :].rearrange("p (a b) -> p a b", a=2), k1[:, 1, :].rearrange("p (a b) -> p a b", a=2)
        sg, u = q1[:, 0, :].rearrange("p (a b) -> p a b", a=2), q1[:, 1, :].rearrange("p (a b) -> p a b", a=2)
        x1g = k1r[:, 0, 0:3 * D].bitcast(f32).rearrange("p (i d) -> p i d", i=3)
        gT = xb[:, :, :].rearrange("p t d -> p (t d)").rearrange("p (a b) -> p a b", a=2)
        lg = sb("lg", [P, 2, E])
        lmax = sb("lmax", [P, 2])
        key = sb("key", [P, 2, E])
        kmax = sb("kmax", [P, 2])
        onehot = sb("onehot", [P, NT, E], bf16)
        before = sb("before", [P, NT + 1, E], bf16)
        over = sb("over", [P, E, E])
        ntile = sb("ntile", [P, E])
        ends = sb("ends", [P, E])
        posf = sb("posf", [P, 2])
        base_bf = sb("base_bf", [1, 2, E], bf16)
        placed = sb("placed", [P, 2, E])
        pos = sb("pos", [P, NT], i32)
        past = sb("past", [P, ROUTED, E])
        npast = sb("npast", [P, ROUTED])
        expert = sb("expert", [P, ROUTED], i32)
        skip = sb("skip", [P, E])
        skipped = sb("skipped", [P, ROUTED, E])
        rowsum = sb("rowsum", [P, ROUTED])
        rowplus = sb("rowplus", [P, ROUTED])
        first_row = sb("first_row", [P, ROUTED], i32)
        xs = sb("xs", [P, 2, PAY])
        ids = sb("ids", [P, ROUTED], i32)
        xT = sb("xT", [P, 2, P])
        x1b = sb("x1b", [P, 2, D])
        res = sb("res", [P, 3, D])

        bank = [ctx.enter_context(nc.psum_tensor(f"bank{i}", [P, 512], f32)) for i in range(8)]

        x_in, mask_in, a_in, b_in, c_in = map(sem, "x_in mask_in a_in b_in c_in".split())
        w1_in, w2_in, b1_in = map(sem, "w1_in w2_in b1_in".split())
        pool_set, dve_step, bot_rdy, table_rdy = map(sem, "pool_set dve_step bot_rdy table_rdy".split())
        masked_rdy, var_rdy, rstd_rdy, xn_rdy = map(sem, "masked_rdy var_rdy rstd_rdy xn_rdy".split())
        ctx_in, kmask_in, qmask_in, masked_in = [[sem(f"{name}{half}") for half in range(2)] for name in
                                                 "ctx_in kmask_in qmask_in masked_in".split()]
        xnT_ps, xnT_rdy, kq_ps, kq_rdy, kqr_rdy, v_ps, v_rdy, bmv_rdy, tg_rdy, xb_rdy = map(
            sem, "xnT_ps xnT_rdy kq_ps kq_rdy kqr_rdy v_ps v_rdy bmv_rdy tg_rdy xb_rdy".split())
        s1_ps, max_rdy, mt_ps, q2_rdy, qbd_rdy, s2_ps, exp_rdy, av_ps, o_rdy = map(
            sem, "s1_ps max_rdy mt_ps q2_rdy qbd_rdy s2_ps exp_rdy av_ps o_rdy".split())
        attn_rdy, proj_ps, var2_rdy, rstd2_rdy, xn2_rdy, xn2T_ps, xn2T_rdy, lg_ps, lg_rdy, hot_rdy = map(
            sem, "attn_rdy proj_ps var2_rdy rstd2_rdy xn2_rdy xn2T_ps xn2T_rdy lg_ps lg_rdy hot_rdy".split())
        rank_ps, total_ps, pos_rdy, expert_rdy, row_rdy, filled, id_rdy, sent, b2t_rdy, x1_rdy, x1_out, maskcol_rdy, col_rdy = map(
            sem, "rank_ps total_ps pos_rdy expert_rdy row_rdy filled id_rdy sent b2t_rdy x1_rdy x1_out maskcol_rdy col_rdy".split())
        oT_ps, norm_rdy, aT_ps = map(sem, "oT_ps norm_rdy aT_ps".split())
        ids_rdy, x1b_rdy, x1g_clear = map(sem, "ids_rdy x1b_rdy x1g_clear".split())
        x1g_in = [sem(f"x1g_in{i}") for i in range(3)]
        xs_in = [sem("xs_in0"), sem("xs_in1")]
        out_done = [sem(f"out_done{i}") for i in range(3)]
        xT_ps, xT_rdy, hg_ps, ha_ps, g_rdy, a_rdy, sg_rdy, u_rdy, gT_ps, gT_rdy, y_ps, fin_rdy = map(
            sem, "xT_ps xT_rdy hg_ps ha_ps g_rdy a_rdy sg_rdy u_rdy gT_ps gT_rdy y_ps fin_rdy".split())

        block = ctx.enter_context(nc.Block())
        STEPS = range(-2, ROUTED + 1)

        def is_tile(i):
            return 0 <= i < ROUTED

        def columns(half):
            return slice(half * 512, half * 512 + 512)

        @block.sync
        def _(sp):
            def load_context(half):
                sp.dma_start(ctx_sb[:, :, columns(half)],
                             ctxT.rearrange("(f p) t -> p f t", p=P)[:, :, columns(half)]).then_inc(ctx_in[half], 16)

            sp.dma_start(x_sb, x.rearrange("(t p) d -> p t d", p=P)).then_inc(x_in, 16)
            sp.dma_start(maskkq[:, 0, columns(0)], key_mask[:, columns(0)]).then_inc(kmask_in[0], 16)
            load_context(0)
            sp.wait_ge(kmask_in[0], 16)
            sp.dma_start(b_sb[:, :], pack_b).then_inc(b_in, 16)
            sp.dma_start(maskkq[:, 1, columns(0)], query_mask[:, columns(0)]).then_inc(qmask_in[0], 16)
            sp.dma_start(maskkq[:, 0, columns(1)], key_mask[:, columns(1)]).then_inc(kmask_in[1], 16)
            sp.dma_start(c_sb[:, :], pack_c).then_inc(c_in, 16)
            load_context(1)
            sp.dma_start(maskkq[:, 1, columns(1)], query_mask[:, columns(1)]).then_inc(qmask_in[1], 16)
            sp.wait_ge(kmask_in[1], 16)
            sp.wait_ge(masked_rdy, 1)
            sp.dma_start(maskkq[HD + 1::HP, 0, columns(1)], masked4[:, columns(1)]).then_inc(masked_in[1], 16)
            sp.dma_start(w1_sb[:, :].rearrange("p (e f) -> p e f", e=E), w1.rearrange("e p f -> p e f")).then_inc(w1_in, 16)
            sp.dma_start(w2_sb[:, :].rearrange("p (e c d) -> p e c d", e=E, c=HC),
                         w2.rearrange("e (c p) d -> p e c d", p=P)).then_inc(w2_in, 16)
            sp.wait_ge(v_rdy, NT)
            sp.wait_ge(kq_rdy, 8)
            sp.wait_ge(xb_rdy, 1)
            sp.dma_start(b1_sb[:, :], b1.rearrange("e f -> (e f)").partition_broadcast(P)).then_inc(b1_in, 16)
            sp.wait_ge(filled, 16)
            sp.dma_start(b2_sb[:, :], b2.rearrange("e f -> (e f)").partition_broadcast(P)).then_inc(b1_in, 16)

            for b in range(B):
                sp.wait_ge(x1_rdy, b + 1)
                sp.dma_start(x1_dram[b * S:(b + 1) * S, :].rearrange("(t p) d -> p t d", p=P),
                             x1[:, 2 * b:2 * b + 2, :]).then_inc(x1_out, 16)

            sp.wait_ge(row_rdy, 1)
            rows = [sp.value_load(first_row[0:1, i:i + 1], min_val=0, max_val=E * N) for i in range(2)]
            sp.wait_ge(sent, 16 * NT)
            for i in range(ROUTED):
                if i >= 2:
                    rows.append(sp.value_load(first_row[0:1, i:i + 1], min_val=0, max_val=E * N))
                    sp.wait_ge(xT_ps, i - 1)
                    sp.wait_ge(ids_rdy, i - 1)
                sp.dma_start(xs[:, i % 2, :], slots[ds(rows[i], P), :]).then_inc(xs_in[i % 2], 16)
            for i in range(3):
                sp.wait_ge(out_done[i], 16 * len(range(i, ROUTED, 3)))

        @block.gpsimd
        def _(pool):
            nc.gpsimd.memset(ones_bf[:, :], 1.0).then_inc(pool_set, 1)
            nc.gpsimd.memset(half_neg[:, :], -0.5).then_inc(pool_set, 1)
            nc.gpsimd.memset(negmax[:, :, :, :, :], 0.0).then_inc(pool_set, 1)
            nc.gpsimd.memset(vpad[:, :, :, HD:HD + 1], 1.0).then_inc(pool_set, 1)
            nc.gpsimd.memset(vpad[:, :, :, HD + 1:HP], 0.0).then_inc(pool_set, 1)
            pool.wait_ge(pool_set, 2)
            for t in (0, 4):
                pool.wait_ge(var_rdy, t // 4 + 1)
                nc.gpsimd.tensor_tensor(rstd[:, t:t + 4], veps[:, t:t + 4], half_neg[:, t:t + 4], ALU.pow).then_inc(rstd_rdy, 1)
            nc.gpsimd.memset(qbd[:, :, :, :, :], 0.0).then_inc(pool_set, 1)
            nc.gpsimd.memset(fill[:, :, 0:D], 0.0).then_inc(pool_set, 1)
            nc.gpsimd.iota(fill[:, :, D:PAY].bitcast(i32), pattern=[[0, FILL_ROWS], [0, 1]], base=NOWHERE,
                           channel_multiplier=0).then_inc(pool_set, 1)
            nc.gpsimd.iota(pay[:, :, D:PAY].bitcast(i32), pattern=[[P, NT], [0, 1]], base=0,
                           channel_multiplier=1).then_inc(id_rdy, 1)
            nc.gpsimd.memset(before[:, 0, :], 0.0).then_inc(pool_set, 1)
            nc.gpsimd.memset(ones_f[:, :], 1.0).then_inc(pool_set, 1)
            pool.wait_ge(a_in, 16)
            nc.gpsimd.tensor_copy(maskcol_sb[:, :], a_sb[:, A_MASK:A_MASK + NT]).then_inc(maskcol_rdy, 1)
            pool.wait_ge(c_in, 16)
            pool.wait_ge(maskcol_rdy, 1)
            nc.gpsimd.tensor_tensor(bmv, bv_sb.unsqueeze(1).broadcast_to([P, NT, D]),
                                    maskcol_sb[:, :].unsqueeze(2).broadcast_to([P, NT, D]), ALU.mult).then_inc(bmv_rdy, 1)
            pool.wait_ge(tg_rdy, 1)
            nc.gpsimd.tensor_scalar(bot[:, :], bo_sb, tg[:, 0:1], None, ALU.mult).then_inc(bot_rdy, 1)
            pool.wait_ge(bot_rdy, 1)
            pool.wait_ge(x_in, 16)
            nc.gpsimd.tensor_tensor(xb[:, :, :], x_sb, bot[:, :].unsqueeze(1).broadcast_to([P, NT, D]), ALU.add).then_inc(xb_rdy, 1)
            pool.wait_ge(pool_set, FILL_SET)
            fills = (E * N + P) // (P * FILL_ROWS)
            pool.dma_start(slots.rearrange("(i p k) d -> p i (k d)", p=P, k=FILL_ROWS),
                           b2_sb[:, 0:FILL_ROWS * PAY].unsqueeze(1).broadcast_to([P, fills, FILL_ROWS * PAY])).then_inc(filled, 16)
            pool.wait_ge(b_in, 16)
            nc.gpsimd.tensor_copy(tri_bf[:, :], b_sb[:, B_TRI:B_TRI + P]).then_inc(pool_set, 1)
            nc.gpsimd.tensor_copy(base_bf[:, :, :], b_sb[0:1, B_ROW:B_ROW + 2 * E].rearrange("p (t e) -> p t e", t=2)
                                  ).then_inc(pool_set, 1)

            def scatter_rows(b):
                pool.wait_ge(pos_rdy, b + 1)
                for t in range(2 * b, 2 * b + 2):
                    pool.indirect_dma_start(out=slots, out_offset=bass.IndirectOffsetOnAxis(ap=pos[:, t:t + 1], axis=0),
                                            in_=pay[:, t, :], in_offset=None).then_inc(sent, 16)

            for b in range(B):
                if b >= 2:
                    scatter_rows(b - 2)
                pool.wait_ge(var2_rdy, b + 1)
                nc.gpsimd.tensor_tensor(rstd2[:, 2 * b:2 * b + 2], veps2[:, 2 * b:2 * b + 2], half_neg[:, 0:2],
                                        ALU.pow).then_inc(rstd2_rdy, 1)
                if b == 0:
                    pool.wait_ge(b1_in, 32)
                    nc.gpsimd.tensor_scalar(b2_sb[:, :], b2_sb[:, :], tg[:, 1:2], None, ALU.mult).then_inc(b2t_rdy, 1)
                    pool.wait_ge(filled, 16)
                    pool.wait_ge(id_rdy, 1)
            scatter_rows(B - 2)
            pool.wait_ge(s1_ps, 2 * B * HG)
            nc.gpsimd.memset(x1g[:, :, :], 0.0).then_inc(x1g_clear, 1)
            scatter_rows(B - 1)
            pool.wait_ge(x1_out, 16 * B)
            pool.wait_ge(x1g_clear, 1)

            for s in STEPS:
                i = s + 1
                if is_tile(i):
                    pool.wait_ge(ids_rdy, i + 1)
                    pool.indirect_dma_start(out=x1g[:, i % 3, :], out_offset=None, in_=x1_dram,
                                            in_offset=bass.IndirectOffsetOnAxis(ap=ids[:, i:i + 1], axis=0),
                                            bounds_check=N - 1, oob_is_err=False).then_inc(x1g_in[i % 3], 16)
                i = s - 1
                if is_tile(i):
                    pool.wait_ge(fin_rdy, i + 1)
                    pool.indirect_dma_start(out=out, out_offset=bass.IndirectOffsetOnAxis(ap=ids[:, i:i + 1], axis=0),
                                            in_=res[:, i % 3, :], in_offset=None, bounds_check=N - 1,
                                            oob_is_err=False).then_inc(out_done[i % 3], 16)

        @block.scalar
        def _(act):
            act.dma_start(mask4[:, :], mask_row.partition_broadcast(HG)).then_inc(mask_in, 16)
            act.wait_ge(pool_set, 1)
            nc.scalar.activation(warm[:, 0:1], ones_bf[0:1, 0:1], ACT.Exp).then_inc(table_rdy, 1)
            act.dma_start(a_sb[:, :], pack_a).then_inc(a_in, 16)
            act.wait_ge(masked_rdy, 1)
            act.wait_ge(kmask_in[0], 16)
            act.dma_start(maskkq[HD + 1::HP, 0, columns(0)], masked4[:, columns(0)]).then_inc(masked_in[0], 16)

            def copy_xnT(half):
                act.wait_ge(xnT_ps, half + 1)
                nc.scalar.activation(xnT[:, columns(half)], bank[XNT_BANK[half]][:, :], ACT.Copy).then_inc(xnT_rdy, 1)

            def round_blocks(first, last):
                for n in range(first, last):
                    side, g, half = BLOCKS[n]
                    src, dst = ((k1, k1r), (q1, q1r))[side]
                    act.wait_ge(kq_rdy, n + 1)
                    nc.scalar.activation(dst[:, g, columns(half)], src[:, g, columns(half)], ACT.Copy).then_inc(kqr_rdy, 1)

            copy_xnT(0)
            round_blocks(0, 4)
            copy_xnT(1)
            act.wait_ge(a_in, 16)
            nc.scalar.activation(tg[:, :], a_sb[:, A_GATES:A_GATES + 2], ACT.Tanh).then_inc(tg_rdy, 1)
            act.wait_ge(pool_set, QBD_SET)

            def spread_queries(b, heads):
                act.wait_ge(q2_rdy, b + 1)
                if b >= 2:
                    act.wait_ge(s2_ps, 8 * (b - 1))
                for j in heads:
                    nc.scalar.activation(qbd[HP * j:HP * (j + 1), b % 2, :, j, :], q2[HP * j:HP * (j + 1), b % 2, :, :],
                                         ACT.Copy).then_inc(qbd_rdy, 1)

            def exponentials(b, g, ns):
                if b >= 1:
                    act.wait_ge(av_ps, 2 * (b - 1) + g + 1)
                for n in ns:
                    st, hf = n // 2, n % 2
                    m = 8 * b + 4 * g + n
                    act.wait_ge(s2_ps, m + 1)
                    nc.scalar.activation(probs[:, g, st, 2 * hf:2 * hf + 2, :].rearrange("p j t -> p (j t)"),
                                         bank[4 + m % 2][:, :], ACT.Exp, scale=HD ** -0.5).then_inc(exp_rdy, 1)

            spread_queries(0, range(HG))
            for b in range(B + 2):
                if b < B:
                    exponentials(b, 0, [0, 1])
                if b == 0:
                    round_blocks(4, 6)
                if b >= 2:
                    act.wait_ge(xn2T_ps, b - 1)
                    nc.scalar.activation(xn2T[:, :], bank[1][:, 0:S], ACT.Copy).then_inc(xn2T_rdy, 1)
                if b < B:
                    exponentials(b, 0, [2, 3])
                if b == 0:
                    round_blocks(6, 8)
                elif b + 1 < B:
                    spread_queries(b + 1, [0, 1])
                if b < B:
                    exponentials(b, 1, [0, 1])
                if b == 0:
                    spread_queries(1, [0, 1])
                if 1 <= b <= B:
                    act.wait_ge(aT_ps, b)
                    if b >= 2:
                        act.wait_ge(proj_ps, b - 1)
                    nc.scalar.activation(attnT[:, :], bank[7][:, 0:S], ACT.Copy).then_inc(attn_rdy, 1)
                if b < B:
                    exponentials(b, 1, [2, 3])
                if b + 1 < B:
                    spread_queries(b + 1, [2, 3])
                if b < B:
                    act.wait_ge(av_ps, 2 * b + 2)
                    if b >= 1:
                        act.wait_ge(oT_ps, b)
                    nc.scalar.activation(o_sb[:, :], bank[6][:, :], ACT.Copy).then_inc(o_rdy, 1)

            nc.scalar.activation(warm[:, 1:2], ones_bf[0:1, 0:1], ACT.Sigmoid).then_inc(table_rdy, 1)

            for s in STEPS:
                i = s + 2
                if is_tile(i):
                    act.wait_ge(xT_ps, i + 1)
                    if i >= 2:
                        act.wait_ge(ha_ps, i - 1)
                    nc.scalar.activation(xT[:, i % 2, :], bank[4][:, 0:P], ACT.Copy).then_inc(xT_rdy, 1)
                i = s + 1
                if is_tile(i):
                    act.wait_ge(g_rdy, i + 1)
                    if i >= 2:
                        act.wait_ge(u_rdy, i - 1)
                    nc.scalar.activation(sg[:, i % 2, :], gsb[:, i % 2, :], ACT.Sigmoid).then_inc(sg_rdy, 1)
                i = s
                if is_tile(i):
                    act.wait_ge(gT_ps, i + 1)
                    if i >= 2:
                        act.wait_ge(y_ps, i - 1)
                    nc.scalar.activation(gT[:, i % 2, :], bank[5][:, :], ACT.Copy).then_inc(gT_rdy, 1)

        @block.vector
        def _(dve):
            linked = [0]

            def link(ins):
                ins.then_inc(dve_step, 1)
                linked[0] += 1
                dve.wait_ge(dve_step, linked[0])

            dve.wait_ge(mask_in, 16)
            nc.vector.tensor_scalar(masked4[:, :], mask4[:, :], 0.0, MASKED, ALU.is_equal, ALU.mult).then_inc(masked_rdy, 1)

            dve.wait_ge(x_in, 16)
            for half in range(2):
                for t in range(4 * half, 4 * half + 4):
                    last = nc.vector.bn_stats(stats[:, t, :], x_sb[:, t, :])
                    if t % 4 < 3:
                        last.then_inc(dve_step, 1)
                        linked[0] += 1
                link(last)
                for t in range(4 * half, 4 * half + 4):
                    last = nc.vector.bn_aggr(mv[:, t, :], stats[:, t, :])
                link(last)
                nc.vector.tensor_scalar(veps[:, 4 * half:4 * half + 4], mv[:, 4 * half:4 * half + 4, 1], EPS, None,
                                        ALU.add).then_inc(var_rdy, 1)

            def keys_queries(n):
                side, g, half = BLOCKS[n]
                cols = columns(half)
                dve.wait_ge(kq_ps, n + 1)
                dve.wait_ge((masked_in, qmask_in)[side][half], 16)
                nc.vector.scalar_tensor_tensor((k1, q1)[side][:, g, cols], bank[KQ_BANK[n]][:, :],
                                               bqk_sb[:, 1 - side, g:g + 1], maskkq[:, side, cols],
                                               ALU.add, ALU.mult).then_inc(kq_rdy, 1)

            def masked_values(half):
                dve.wait_ge(bmv_rdy, 1)
                dve.wait_ge(v_ps, half + 1)
                for t in range(4 * half, 4 * half + 4):
                    nc.vector.scalar_tensor_tensor(vpad[:, t, :, 0:HD],
                                                   bank[V_BANK[t // 4]][:, t % 4 * D:t % 4 * D + D].rearrange("p (h d) -> p h d", h=H),
                                                   maskcol_sb[:, t:t + 1], bmv[:, t, :].rearrange("p (h d) -> p h d", h=H),
                                                   ALU.mult, ALU.add).then_inc(v_rdy, 1)

            def maxima(b, g, heads=range(HG)):
                if b >= 2 and g == 0:
                    dve.wait_ge(mt_ps, b - 1)
                for j in heads:
                    dve.wait_ge(s1_ps, (2 * b + g) * HG + j + 1)
                    nc.vector.tensor_reduce(negmax[:, b % 2, g, :, HP * j + HD], bank[j][:, :].rearrange("p (t s) -> p t s", t=2),
                                            AX.X, ALU.max, negate=True).then_inc(max_rdy, 1)

            def shift_queries(b):
                dve.wait_ge(mt_ps, b + 1)
                if b >= 2:
                    dve.wait_ge(qbd_rdy, HG * (b - 1))
                nc.vector.tensor_tensor(q2[:, b % 2, :, :], q1[:, :, b * S:(b + 1) * S],
                                        bank[3][:, :].rearrange("p (g t) -> p g t", g=G), ALU.add).then_inc(q2_rdy, 1)

            def normalise(b):
                dve.wait_ge(oT_ps, b + 1)
                o = bank[7][:, :].rearrange("p (n j c) -> p n j c", n=4, j=HG)
                link(nc.vector.reciprocal(rec[:, :, :], o[:, :, :, HD]))
                if b >= 1:
                    dve.wait_ge(aT_ps, b)
                for g in range(G):
                    nc.vector.tensor_tensor(attn[:, :, g, :].rearrange("p t (j d) -> p t j d", j=HG),
                                            o[:, 2 * g:2 * g + 2, :, 0:HD],
                                            rec[:, 2 * g:2 * g + 2, :].unsqueeze(3).broadcast_to([P, 2, HG, HD]),
                                            ALU.mult).then_inc(norm_rdy, 1)

            def residual(b):
                dve.wait_ge(proj_ps, b + 1)
                dve.wait_ge(xb_rdy, 1)
                nc.vector.scalar_tensor_tensor(x1[:, 2 * b:2 * b + 2, :],
                                               bank[7][:, 0:2 * D].rearrange("p (t d) -> p t d", t=2), tg[:, 0:1],
                                               xb[:, 2 * b:2 * b + 2, :], ALU.mult, ALU.add).then_inc(x1_rdy, 1)
                dve.wait_ge(x1_rdy, b + 1)
                nc.vector.bn_stats(stats2[:, 2 * b, :], x1[:, 2 * b, :]).then_inc(dve_step, 1)
                linked[0] += 1
                link(nc.vector.bn_stats(stats2[:, 2 * b + 1, :], x1[:, 2 * b + 1, :]))
                nc.vector.bn_aggr(mv2[:, 2 * b, :], stats2[:, 2 * b, :])
                link(nc.vector.bn_aggr(mv2[:, 2 * b + 1, :], stats2[:, 2 * b + 1, :]))
                nc.vector.tensor_scalar(veps2[:, 2 * b:2 * b + 2], mv2[:, 2 * b:2 * b + 2, 1], EPS, None,
                                        ALU.add).then_inc(var2_rdy, 1)

            def second_norm(b):
                dve.wait_ge(rstd2_rdy, b + 1)
                for t in range(2 * b, 2 * b + 2):
                    nc.vector.tensor_scalar(pay[:, t, 0:D], x1[:, t, :], mv2[:, t, 0:1], rstd2[:, t:t + 1],
                                            ALU.subtract, ALU.mult).then_inc(xn2_rdy, 1)

            def route(b):
                dve.wait_ge(lg_ps, b + 1)
                nc.vector.tensor_tensor(lg[:, :, :], bank[2][:, 0:2 * E].rearrange("p (t e) -> p t e", t=2),
                                        rb_sb[:, :].unsqueeze(1).broadcast_to([P, 2, E]), ALU.add).then_inc(lg_rdy, 1)
                dve.wait_ge(lg_rdy, b + 1)
                link(nc.vector.tensor_reduce(lmax[:, :], lg[:, :, :], AX.X, ALU.max))
                for t in range(2):
                    last = nc.vector.scalar_tensor_tensor(key[:, t, :], lg[:, t, :], lmax[:, t:t + 1], b_sb[:, B_PRI:B_PRI + E],
                                                          ALU.is_equal, ALU.mult)
                link(last)
                link(nc.vector.tensor_reduce(kmax[:, :], key[:, :, :], AX.X, ALU.max))
                nc.vector.tensor_tensor(onehot[:, 2 * b:2 * b + 2, :], key[:, :, :],
                                        kmax[:, :].unsqueeze(2).broadcast_to([P, 2, E]), ALU.is_equal).then_inc(hot_rdy, 1)

            def places(b):
                dve.wait_ge(hot_rdy, b + 1)
                for t in range(2 * b, 2 * b + 2):
                    nc.vector.tensor_tensor(before[:, t + 1, :], before[:, t, :], onehot[:, t, :], ALU.add).then_inc(col_rdy, 1)
                    dve.wait_ge(col_rdy, t + 1)
                dve.wait_ge(rank_ps, b + 1)
                link(nc.vector.tensor_tensor(placed[:, :, :], bank[2][:, 32:32 + 2 * E].rearrange("p (t e) -> p t e", t=2), onehot[:, 2 * b:2 * b + 2, :], ALU.mult))
                link(nc.vector.tensor_reduce(posf[:, :], placed[:, :, :], AX.X, ALU.add))
                nc.vector.tensor_copy(pos[:, 2 * b:2 * b + 2], posf[:, :]).then_inc(pos_rdy, 1)

            dve.wait_ge(a_in, 16)
            for half in range(2):
                dve.wait_ge(rstd_rdy, half + 1)
                for t in range(4 * half, 4 * half + 4):
                    nc.vector.tensor_scalar(xn[:, t, :], x_sb[:, t, :], mv[:, t, 0:1], rstd[:, t:t + 1],
                                            ALU.subtract, ALU.mult).then_inc(xn_rdy, 1)
            for n in range(3):
                keys_queries(n)
            dve.wait_ge(pool_set, VPAD_SET)
            maxima(0, 0, [0, 1])
            keys_queries(3)
            maxima(0, 0, [2, 3])
            maxima(0, 1)
            keys_queries(4)
            shift_queries(0)
            keys_queries(5)
            maxima(1, 0)
            masked_values(0)
            maxima(1, 1)
            keys_queries(6)
            dve.wait_ge(b_in, 16)
            for b in range(B + 2):
                if b >= 2 and b != B:
                    route(b - 2)
                if b + 1 < B:
                    shift_queries(b + 1)
                if b == 0:
                    keys_queries(7)
                if 1 <= b <= B:
                    normalise(b - 1)
                if 2 <= b and b != B:
                    places(b - 2)
                if b + 2 < B:
                    maxima(b + 2, 0)
                if b == 0:
                    masked_values(1)
                if b == B:
                    route(b - 2)
                if 1 <= b <= B:
                    residual(b - 1)
                if b == B:
                    places(b - 2)
                if b + 2 < B:
                    maxima(b + 2, 1, [0, 1])
                if 1 <= b <= B:
                    second_norm(b - 1)
                if b + 2 < B:
                    maxima(b + 2, 1, [2, 3])

            total = bank[0][:, 0:E]
            dve.wait_ge(total_ps, 1)
            link(nc.vector.tensor_tensor(over[:, :, :], total.unsqueeze(2).broadcast_to([P, E, E]),
                                         b_sb[:, B_THR:B_THR + E * E].rearrange("p (e k) -> p e k", e=E), ALU.is_gt))
            link(nc.vector.tensor_reduce(ntile[:, :], over[:, :, :], AX.X, ALU.add))
            nc.vector.tensor_scalar(skip[:, :], ntile[:, :], -float(P), float(N), ALU.mult, ALU.add).then_inc(dve_step, 1)
            linked[0] += 1
            link(nc.vector.tensor_tensor_scan(ends[:, :], ones_f[:, :], ntile[:, :], 0.0, ALU.mult, ALU.add))
            link(nc.vector.tensor_tensor(past[:, :, :], ends[:, :].unsqueeze(1).broadcast_to([P, ROUTED, E]),
                                         b_sb[:, B_TILE:B_TROW].rearrange("p (i e) -> p i e", i=ROUTED), ALU.is_le))
            link(nc.vector.tensor_tensor(skipped[:, :, :], past[:, :, :], skip[:, :].unsqueeze(1).broadcast_to([P, ROUTED, E]),
                                         ALU.mult))
            link(nc.vector.tensor_reduce(rowsum[:, :], skipped[:, :, :], AX.X, ALU.add))
            link(nc.vector.tensor_tensor(rowplus[:, :], rowsum[:, :], b_sb[:, B_TROW:B_END], ALU.add))
            nc.vector.tensor_scalar(first_row[:, :], rowplus[:, :], float(E * N), None, ALU.min).then_inc(row_rdy, 1)
            link(nc.vector.tensor_reduce(npast[:, :], past[:, :, :], AX.X, ALU.add))
            nc.vector.tensor_scalar(expert[:, :], npast[:, :], float(E - 1), None, ALU.min).then_inc(expert_rdy, 1)
            dve.wait_ge(expert_rdy, 1)
            dve.wait_ge(b2t_rdy, 1)

            def dve_expert(i):
                return dve.value_load(expert[0:1, i:i + 1], min_val=0, max_val=E - 1)

            e = [dve_expert(0)]
            for s in STEPS:
                i = s + 2
                if is_tile(i):
                    dve.wait_ge(xs_in[i % 2], 16 * (i // 2 + 1))
                    nc.vector.tensor_copy(ids[:, ds(i, 1)], xs[:, i % 2, D:PAY].bitcast(i32)).then_inc(ids_rdy, 1)
                i = s + 1
                if is_tile(i):
                    if i == 0:
                        dve.wait_ge(b1_in, 32)
                    dve.wait_ge(hg_ps, i + 1)
                    nc.vector.tensor_tensor(gsb[:, i % 2, :], bank[2 * (i % 2)][:, :],
                                            b1_sb[:, ds(e[i] * (2 * HID) + HID, HID)], ALU.add).then_inc(g_rdy, 1)
                    dve.wait_ge(ha_ps, i + 1)
                    nc.vector.tensor_tensor(asb[:, i % 2, :], bank[2 * (i % 2) + 1][:, :],
                                            b1_sb[:, ds(e[i] * (2 * HID), HID)], ALU.add).then_inc(a_rdy, 1)
                    if i + 1 < ROUTED:
                        e.append(dve_expert(i + 1))
                    dve.wait_ge(a_rdy, i + 1)
                    dve.wait_ge(sg_rdy, i + 1)
                    if i >= 2:
                        dve.wait_ge(gT_ps, i - 1)
                    nc.vector.tensor_tensor(u[:, i % 2, :], asb[:, i % 2, :], sg[:, i % 2, :], ALU.mult).then_inc(u_rdy, 1)
                i = s - 1
                if is_tile(i):
                    dve.wait_ge(x1g_in[i % 3], 16 * (i // 3 + 1))
                    nc.vector.tensor_tensor(x1b[:, i % 2, :], x1g[:, i % 3, :], b2_sb[:, ds(e[i] * D, D)],
                                            ALU.add).then_inc(x1b_rdy, 1)
                    dve.wait_ge(y_ps, i + 1)
                    if i >= 3:
                        dve.wait_ge(out_done[i % 3], 16 * (i // 3))
                    dve.wait_ge(x1b_rdy, i + 1)
                    nc.vector.scalar_tensor_tensor(res[:, i % 3, :], bank[6 + i % 2][:, 0:D], tg[:, 1:2],
                                                   x1b[:, i % 2, :], ALU.mult, ALU.add).then_inc(fin_rdy, 1)

        @block.tensor
        def _(pe):
            def warm_up(products):
                for n in range(products):
                    nc.tensor.matmul(bank[5][:, 0:P], ones_bf[:, :], ones_bf[:, :], start=True, stop=True)

            pe.wait_ge(pool_set, 1)
            warm_up(WARM_UP)
            def project(n):
                side, g, half = BLOCKS[n]
                cols = columns(half)
                if side == 0:
                    for f in range(2):
                        mm = nc.tensor.matmul(bank[KQ_BANK[n]][:, :], wk_sb[:, f, g * P:(g + 1) * P], ctx_sb[:, f, cols],
                                              start=f == 0, stop=f == 1)
                else:
                    mm = nc.tensor.matmul(bank[KQ_BANK[n]][:, :], wq_sb[:, g * P:(g + 1) * P], xnT[:, cols], start=True, stop=True)
                mm.then_inc(kq_ps, 1)

            def transpose_xn(half):
                for t in range(4 * half, 4 * half + 4):
                    pe.wait_ge(xn_rdy, t + 1)
                    mm = nc.tensor.transpose(bank[XNT_BANK[half]][:, t % 4 * P:t % 4 * P + P], xn[:, t, :], ident)
                mm.then_inc(xnT_ps, 1)

            def project_values(half):
                pe.wait_ge(kq_rdy, (3, 8)[half])
                for t in range(4 * half, 4 * half + 4):
                    for f in range(2):
                        mm = nc.tensor.matmul(bank[V_BANK[half]][:, t % 4 * D:t % 4 * D + D], ctx_sb[:, f, t * P:(t + 1) * P],
                                              wv_sb[:, f, :], start=f == 0, stop=f == 1)
                mm.then_inc(v_ps, 1)

            pe.wait_ge(a_in, 16)
            pe.wait_ge(ctx_in[0], 16)
            project(0)
            transpose_xn(0)
            pe.wait_ge(b_in, 16)
            pe.wait_ge(xnT_rdy, 1)
            project(1)
            project(2)

            def scores_for_max(b, groups=range(G)):
                for g in groups:
                    n = 2 * b + g
                    for tt in range(2):
                        for j in range(HG):
                            if tt == 0 and n >= 1:
                                pe.wait_ge(max_rdy, (n - 1) * HG + j + 1)
                            if tt == 0 and g == 0 and j == 2 and b >= 4:
                                pe.wait_ge(pos_rdy, b - 3)
                            if tt == 0 and g == 0 and j == 3 and b >= 1:
                                pe.wait_ge(q2_rdy, b)
                            q0 = b * S + tt * P
                            mm = nc.tensor.matmul(bank[j][:, tt * S:(tt + 1) * S], q1r[HP * j:HP * (j + 1), g, q0:q0 + P],
                                                  k1r[HP * j:HP * (j + 1), g, b * S:(b + 1) * S], start=True, stop=True)
                            if tt == 1:
                                mm.then_inc(s1_ps, 1)

            def transpose_max(b):
                pe.wait_ge(max_rdy, 2 * HG * (b + 1))
                for g in range(G):
                    for tt in range(2):
                        c = (2 * g + tt) * P
                        mm = nc.tensor.transpose(bank[3][:, c:c + P], negmax[:, b % 2, g, tt, :], ident)
                mm.then_inc(mt_ps, 1)

            def scores(b, g, ns):
                for n in ns:
                    st, hf = n // 2, n % 2
                    pe.wait_ge(qbd_rdy, HG * b + 2 * hf + 2)
                    m = 8 * b + 4 * g + n
                    if m >= 2:
                        pe.wait_ge(exp_rdy, m - 1)
                    k0 = b * S + st * P
                    nc.tensor.matmul(bank[4 + m % 2][:, :], k1[:, g, k0:k0 + P],
                                     qbd[:, b % 2, g, 2 * hf:2 * hf + 2, :].rearrange("p j t -> p (j t)"),
                                     start=True, stop=True).then_inc(s2_ps, 1)

            def values(b, g):
                if g == 0 and b >= 1:
                    pe.wait_ge(o_rdy, b)
                for st in range(2):
                    pe.wait_ge(exp_rdy, 8 * b + 4 * g + 2 * st + 2)
                    for j in range(HG):
                        mm = nc.tensor.matmul(bank[6][HP * j:HP * (j + 1), g * S:(g + 1) * S], vpad[:, 2 * b + st, HG * g + j, :],
                                              probs[:, g, st, j, :], start=st == 0, stop=st == 1)
                mm.then_inc(av_ps, 1)

            def transpose_output(b):
                pe.wait_ge(o_rdy, b + 1)
                if b >= 1:
                    pe.wait_ge(x1_rdy, b)
                else:
                    pe.wait_ge(v_rdy, NT)
                for n in range(4):
                    mm = nc.tensor.transpose(bank[7][:, n * P:(n + 1) * P], o_sb[:, n * P:(n + 1) * P], ident)
                mm.then_inc(oT_ps, 1)

            def transpose_attention(b):
                pe.wait_ge(norm_rdy, 2 * (b + 1))
                for tt in range(2):
                    mm = nc.tensor.transpose(bank[7][:, tt * P:(tt + 1) * P], attn[:, tt, :, :].rearrange("p g c -> p (g c)"), ident)
                mm.then_inc(aT_ps, 1)

            def output_projection(b):
                pe.wait_ge(attn_rdy, b + 1)
                for tt in range(2):
                    t0 = b * S + tt * P
                    o = bank[7][:, tt * D:(tt + 1) * D]
                    nc.tensor.matmul(o, xnT[:, t0:t0 + P], wox_sb, start=True, stop=False)
                    mm = nc.tensor.matmul(o, attnT[:, tt * P:(tt + 1) * P], woa_sb, start=False, stop=True)
                mm.then_inc(proj_ps, 1)

            def transpose_norm(b):
                pe.wait_ge(xn2_rdy, 2 * (b + 1))
                pe.wait_ge(max_rdy, 2 * HG * min(b + 4, B) - 2)
                for tt in range(2):
                    mm = nc.tensor.transpose(bank[1][:, tt * P:tt * P + P], pay[:, 2 * b + tt, 0:D], ident)
                mm.then_inc(xn2T_ps, 1)

            def router(b):
                pe.wait_ge(xn2T_rdy, b + 1)
                pe.wait_ge(max_rdy, 2 * HG * min(b + 4, B))
                for tt in range(2):
                    mm = nc.tensor.matmul(bank[2][:, tt * E:(tt + 1) * E], xn2T[:, tt * P:(tt + 1) * P], rw_sb,
                                          start=True, stop=True)
                mm.then_inc(lg_ps, 1)

            def ranks(b):
                pe.wait_ge(pool_set, ALL_SET)
                pe.wait_ge(lg_rdy, b + 1)
                r = bank[2][:, 32:32 + 2 * E].rearrange("p (t e) -> p t e", t=2)
                nc.tensor.matmul(r, ones_bf[0:1, :], base_bf[0:1, :, :], start=True, stop=False)
                if b >= 1:
                    pe.wait_ge(col_rdy, 2 * b)
                nc.tensor.matmul(r, ones_bf[:, :], before[:, 2 * b, :].unsqueeze(1).broadcast_to([P, 2, E]), start=False, stop=False)
                pe.wait_ge(hot_rdy, b + 1)
                nc.tensor.matmul(r[:, 1, :], ones_bf[:, :], onehot[:, 2 * b, :], start=False, stop=False)
                nc.tensor.matmul(r, tri_bf[:, :], onehot[:, 2 * b:2 * b + 2, :], start=False, stop=True).then_inc(rank_ps, 1)
                if b == B - 1:
                    pe.wait_ge(col_rdy, NT)
                    nc.tensor.matmul(bank[0][:, 0:E], ones_bf[:, :], before[:, NT, :], start=True, stop=True).then_inc(total_ps, 1)

            pe.wait_ge(kqr_rdy, 2)
            scores_for_max(0, [0])
            project(3)
            transpose_xn(1)
            pe.wait_ge(ctx_in[1], 16)
            project(4)
            pe.wait_ge(kqr_rdy, 4)
            scores_for_max(0, [1])
            pe.wait_ge(c_in, 16)
            project_values(0)
            pe.wait_ge(kq_rdy, 4)
            pe.wait_ge(xnT_rdy, 2)
            project(5)
            transpose_max(0)
            scores_for_max(1, [0])
            pe.wait_ge(kq_rdy, 5)
            for b in range(B):
                scores(b, 0, [0, 1])
                if b == 0:
                    scores_for_max(1, [1])
                    pe.wait_ge(kq_rdy, 6)
                    project(6)
                if b >= 2:
                    transpose_norm(b - 2)
                scores(b, 0, [2])
                if b >= 2:
                    router(b - 2)
                scores(b, 0, [3])
                if b + 1 < B:
                    transpose_max(b + 1)
                if b == 0:
                    pe.wait_ge(kq_rdy, 7)
                    project(7)
                else:
                    transpose_output(b - 1)
                pe.wait_ge(v_rdy, NT if b >= 2 else NT // 2)
                values(b, 0)
                if b >= 2:
                    ranks(b - 2)
                scores(b, 1, [0, 1])
                if b >= 1:
                    transpose_attention(b - 1)
                if b == 0:
                    pe.wait_ge(kqr_rdy, 8)
                if b + 2 < B:
                    scores_for_max(b + 2, [0])
                scores(b, 1, [2, 3])
                if b == 0:
                    project_values(1)
                if b >= 1:
                    output_projection(b - 1)
                values(b, 1)
                if b + 2 < B:
                    scores_for_max(b + 2, [1])

            warm_up(8)
            transpose_output(B - 1)
            transpose_norm(B - 2)
            transpose_attention(B - 1)
            router(B - 2)
            output_projection(B - 1)
            ranks(B - 2)
            warm_up(10)
            transpose_norm(B - 1)
            router(B - 1)
            ranks(B - 1)
            warm_up(FFN_WARM_UP)

            def pe_expert(i):
                return pe.value_load(expert[0:1, i:i + 1], min_val=0, max_val=E - 1)

            pe.wait_ge(w1_in, 16)
            pe.wait_ge(expert_rdy, 1)
            e = [pe_expert(0)]
            def transpose_rows(i):
                pe.wait_ge(xs_in[i % 2], 16 * (i // 2 + 1))
                if i >= 1:
                    pe.wait_ge(xT_rdy, i)
                nc.tensor.transpose(bank[4][:, 0:P], xs[:, i % 2, 0:D], ident).then_inc(xT_ps, 1)

            def hidden_layer(i):
                pe.wait_ge(xT_rdy, i + 1)
                if i >= 2:
                    pe.wait_ge(a_rdy, i - 1)
                nc.tensor.matmul(bank[2 * (i % 2)][:, :], xT[:, i % 2, :], w1_sb[:, ds(e[i] * (2 * HID) + HID, HID)],
                                 start=True, stop=True).then_inc(hg_ps, 1)
                nc.tensor.matmul(bank[2 * (i % 2) + 1][:, :], xT[:, i % 2, :], w1_sb[:, ds(e[i] * (2 * HID), HID)],
                                 start=True, stop=True).then_inc(ha_ps, 1)
                if i + 1 < ROUTED:
                    e.append(pe_expert(i + 1))

            transpose_rows(0)
            transpose_rows(1)
            hidden_layer(0)
            for s in range(ROUTED + 1):
                if is_tile(s + 2):
                    transpose_rows(s + 2)
                if is_tile(s + 1):
                    hidden_layer(s + 1)
                i = s
                if is_tile(i):
                    pe.wait_ge(u_rdy, i + 1)
                    if i >= 1:
                        pe.wait_ge(gT_rdy, i)
                    for c in range(HC):
                        mm = nc.tensor.transpose(bank[5][:, c * P:(c + 1) * P], u[:, i % 2, c * P:(c + 1) * P], ident)
                    mm.then_inc(gT_ps, 1)
                i = s - 1
                if is_tile(i):
                    if i == 0:
                        pe.wait_ge(w2_in, 16)
                    pe.wait_ge(gT_rdy, i + 1)
                    if i >= 2:
                        pe.wait_ge(fin_rdy, i - 1)
                    for c in range(HC):
                        mm = nc.tensor.matmul(bank[6 + i % 2][:, 0:D], gT[:, i % 2, c * P:(c + 1) * P],
                                              w2_sb[:, ds(e[i] * (HC * D) + c * D, D)], start=c == 0, stop=c == HC - 1)
                    mm.then_inc(y_ps, 1)


BLOCKS = [(0, 0, 0), (1, 0, 0), (0, 1, 0), (1, 1, 0), (0, 0, 1), (1, 0, 1), (0, 1, 1), (1, 1, 1)]
KQ_BANK = [4, 5, 6, 7, 5, 7, 7, 7]
XNT_BANK = [0, 4]
V_BANK = [6, 7]


def pad_heads(a):
    import numpy as np
    a = a.reshape(a.shape[:-1] + (H, HD))
    return np.concatenate([a, np.zeros(a.shape[:-1] + (HP - HD,), a.dtype)], -1).reshape(a.shape[:-2] + (H * HP,))


def shape_constants():
    import numpy as np
    f = np.float32
    c = np.zeros((P, B_END - B_TRI), f)
    o = -B_TRI
    c[:, o + B_TRI:o + B_TRI + P] = np.triu(np.ones((P, P), f), 1)
    c[:, o + B_THR:o + B_THR + E * E] = np.tile(np.arange(E) * P, E)
    c[:, o + B_PRI:o + B_PRI + E] = E - np.arange(E)
    c[:, o + B_ROW:o + B_ROW + 2 * E] = np.tile(np.arange(E) * N, 2)
    c[:, o + B_TILE:o + B_TROW] = np.repeat(np.arange(ROUTED), E)
    c[:, o + B_TROW:o + B_END] = np.arange(ROUTED) * P
    return c


def kernel(x, ctx_2048, mask_BxS2_fk1, g_xattn, g_ffn, L0_xattn_W_src, L0_xattn_b_src, L0_xattn_W_tgt, L0_xattn_b_tgt,
           L0_xattn_W_out, L0_xattn_b_out, L0_ffn_router_w, L0_ffn_router_b, L0_ffn_w1, L0_ffn_b1, L0_ffn_w2, L0_ffn_b2):
    import numpy as np
    import concourse.bacc as bacc
    from concourse.bass_utils import run_bass_kernel_spmd as run

    a = np.asarray
    consts = shape_constants()
    mask = a(mask_BxS2_fk1).reshape(1, N)
    w_src, b_src, w_out = a(L0_xattn_W_src), a(L0_xattn_b_src), a(L0_xattn_W_out)
    row = np.arange(P) % HP
    key_mask, query_mask = np.zeros((P, N), np.float32), np.zeros((P, N), np.float32)
    key_mask[row < HD], key_mask[row == HD] = mask, 1
    query_mask[row < HD], query_mask[row == HD + 1] = mask, 1
    bq = pad_heads(a(L0_xattn_b_tgt)).reshape(G, P).T.copy()
    bk = pad_heads(b_src[:D]).reshape(G, P).T.copy()
    bq[row == HD + 1] = 1
    bk[(row == HD) | (row == HD + 1)] = 1

    def by_rows(m):
        return m.reshape(-1, P, m.shape[1]).transpose(1, 0, 2).reshape(P, -1)

    def on_all(v):
        return np.broadcast_to(v, (P, v.size))

    arrays = {
        "x": a(x).reshape(N, D),
        "ctxT": a(ctx_2048).reshape(N, F).T,
        "mask_row": mask.reshape(N), "key_mask": key_mask, "query_mask": query_mask,
        "pack_a": np.concatenate([np.eye(P, dtype=np.float32), by_rows(pad_heads(w_src[:D].T)), bq, bk, mask.reshape(NT, P).T,
                                  on_all(a(g_xattn)), on_all(a(g_ffn))], 1),
        "pack_b": np.concatenate([pad_heads(a(L0_xattn_W_tgt).T), a(L0_ffn_router_w),
                                  on_all(a(L0_ffn_router_b)), consts], 1),
        "pack_c": np.concatenate([by_rows(w_src[D:].T), w_out[:, :D].T, w_out[:, D:].T, on_all(b_src[D:]),
                                  on_all(a(L0_xattn_b_out))], 1),
        "w1": a(L0_ffn_w1), "b1": a(L0_ffn_b1), "w2": a(L0_ffn_w2), "b2": a(L0_ffn_b2),
    }
    nc = bacc.Bacc("TRN2", target_bir_lowering=False, num_devices=1)
    arrays = {f"in_{k}": np.ascontiguousarray(v) for k, v in arrays.items()}
    args = [nc.dram_tensor(k, v.shape, mybir.dt.from_np(v.dtype), kind="ExternalInput").ap() for k, v in arrays.items()]
    out = nc.dram_tensor("out_0", (N, D), mybir.dt.float32, kind="ExternalOutput").ap()
    build(nc, *args, out)
    r = run(nc, [arrays], core_ids=[0])
    return np.asarray(r.results[0]["out_0"]).reshape(B, S, D)
```
